# Optimizing a Trainium2 kernel written in Bass

```python
import numpy as np
import jax
import jax.numpy as jnp

def _softmax(x, axis=-1):
    return jax.nn.softmax(x, axis=axis)

def _gelu(x):
    return jax.nn.gelu(x, approximate=True)

def _silu(x):
    return jax.nn.silu(x)

def _sigmoid(x):
    return jax.nn.sigmoid(x)

def _layernorm(x, axis=-1, eps=1e-05):
    m = jnp.mean(x, axis=axis, keepdims=True)
    v = jnp.var(x, axis=axis, keepdims=True)
    return (x - m) / jnp.sqrt(v + eps)

def _scatter_add(tgt, idx, src, axis=0):
    return tgt.at[idx].add(src)

def _segment_sum(src, seg, n):
    return jax.ops.segment_sum(src, seg, n)
kernel_name = 'mk_gps_d2_gnn_r16_015d8a'

def setup_inputs(seed: int=0):
    np.random.seed(seed)
    _w = jnp.asarray

    def _rec_inputs():
        import jax
        import jax.numpy as jnp
        _gk = jax.random.key(seed)
        x = -0.0002117 + 1 * jax.random.normal(jax.random.fold_in(_gk, 1), (6250, 256), jnp.float32)
        src = jax.random.randint(jax.random.fold_in(_gk, 2), (100000,), 0, 6250, jnp.int32)
        dst = jnp.minimum((6250 * jax.random.uniform(jax.random.fold_in(_gk, 3), (100000,)) ** 2.0).astype(jnp.int32), 99999)
        _o = jnp.argsort(dst, stable=True)
        src = src[_o]
        dst = dst[_o]
        edge_weight = jax.random.uniform(jax.random.fold_in(_gk, 14), (100000,), jnp.float32, 0.0, 0.999998)
        return (x, src, dst, edge_weight)
    x, src, dst, edge_weight = _rec_inputs()

    def _L0_gnn_setup():
        import jax, jax.numpy as jnp
        import numpy as np
        N, D, E = (6250, 256, 312500)
        H = 2 * D
        EPS = 0.0
        key = jax.random.key(seed)
        k1, k2, k3, k4, k5, k6, k7 = jax.random.split(key, 7)
        x = jax.random.normal(k1, (N, D), dtype=jnp.float32)
        edge_index = jax.random.randint(k2, (2, E), 0, N, dtype=jnp.int64)
        edge_weight = jax.random.uniform(k3, (E,), dtype=jnp.float32)
        s1 = 1.0 / np.sqrt(D)
        s2 = 1.0 / np.sqrt(H)
        W1 = jax.random.uniform(k4, (D, H), dtype=jnp.float32, minval=-s1, maxval=s1)
        b1 = jax.random.uniform(k5, (H,), dtype=jnp.float32, minval=-s1, maxval=s1)
        W2 = jax.random.uniform(k6, (H, D), dtype=jnp.float32, minval=-s2, maxval=s2)
        b2 = jax.random.uniform(k7, (D,), dtype=jnp.float32, minval=-s2, maxval=s2)
        return {'x': x, 'edge_index': edge_index, 'edge_weight': edge_weight, 'W1': W1, 'b1': b1, 'W2': W2, 'b2': b2}
    _L0_gnn_all = _L0_gnn_setup()
    _L0_gnn_in = {k: v for k, v in _L0_gnn_all.items() if k in ('W1', 'b1', 'W2', 'b2')}
    del _L0_gnn_all

    def _L0_mix_setup():
        import jax, jax.numpy as jnp
        import numpy as np
        NHEAD = 8
        ATT_EPS = 1e-06
        LN_EPS = 1e-05

        def _layernorm(x, g, b):
            mu = jnp.mean(x, axis=-1, keepdims=True)
            var = jnp.mean(jnp.square(x - mu), axis=-1, keepdims=True)
            return (x - mu) * jax.lax.rsqrt(var + LN_EPS) * g + b
        key = jax.random.key(seed)
        ks = jax.random.split(key, 7)
        N, L, C = (4, 1024, 256)
        s = 1.0 / np.sqrt(C)
        return {'x': jax.random.normal(ks[0], (N, L, C), jnp.float32), 'Wq': jax.random.normal(ks[1], (C, C), jnp.float32) * s, 'Wk': jax.random.normal(ks[2], (C, C), jnp.float32) * s, 'Wv': jax.random.normal(ks[3], (C, C), jnp.float32) * s, 'Wm': jax.random.normal(ks[4], (C, C), jnp.float32) * s, 'W1': jax.random.normal(ks[5], (2 * C, 2 * C), jnp.float32) * (1.0 / np.sqrt(2 * C)), 'W2': jax.random.normal(ks[6], (2 * C, C), jnp.float32) * (1.0 / np.sqrt(2 * C)), 'g1': jnp.ones((C,), jnp.float32), 'b1': jnp.zeros((C,), jnp.float32), 'g2': jnp.ones((C,), jnp.float32), 'b2': jnp.zeros((C,), jnp.float32)}
    _L0_mix_all = _L0_mix_setup()
    _L0_mix_in = {k: v for k, v in _L0_mix_all.items() if k in ('Wq', 'Wk', 'Wv', 'Wm', 'W1', 'W2', 'g1', 'b1', 'g2', 'b2')}
    del _L0_mix_all

    def _L0_ffn_setup():
        import jax, jax.numpy as jnp
        import numpy as np
        B, K, D = (512, 16, 256)
        E = 32
        H = int(D * 0.25)
        key = jax.random.key(seed)
        ks = jax.random.split(key, 7)
        d_rs = D ** (-0.5)
        h_rs = H ** (-0.5)
        x = jax.random.normal(ks[0], (B, K, D), dtype=jnp.float32)
        router_w = jax.random.uniform(ks[1], (E, D), jnp.float32, -d_rs, d_rs)
        router_b = jax.random.uniform(ks[2], (E,), jnp.float32, -d_rs, d_rs)
        W1 = jax.random.uniform(ks[3], (E, D, H), jnp.float32, -h_rs, h_rs)
        b1 = jax.random.uniform(ks[4], (E, H), jnp.float32, -h_rs, h_rs)
        W2 = jax.random.uniform(ks[5], (E, H, D), jnp.float32, -d_rs, d_rs)
        b2 = jax.random.uniform(ks[6], (E, D), jnp.float32, -d_rs, d_rs)
        return {'x': x, 'router_w': router_w, 'router_b': router_b, 'W1': W1, 'b1': b1, 'W2': W2, 'b2': b2}
    _L0_ffn_all = _L0_ffn_setup()
    _L0_ffn_in = {k: v for k, v in _L0_ffn_all.items() if k in ('router_w', 'router_b', 'W1', 'b1', 'W2', 'b2')}
    del _L0_ffn_all

    def _L1_gnn_setup():
        import jax, jax.numpy as jnp
        import numpy as np
        N = 12500
        E = 37500
        C = 256
        key = jax.random.key(seed)
        k1, k2, k3, k4, k5 = jax.random.split(key, 5)
        x = jax.random.normal(k1, (N, C), dtype=jnp.float32)
        sources = jax.random.randint(k2, (E,), 0, N, dtype=jnp.int64)
        targets = jax.random.randint(k3, (E,), 0, N, dtype=jnp.int64)
        norm = jax.random.uniform(k4, (N, 1), dtype=jnp.float32)
        std = float(np.sqrt(2.0 / (C + C)))
        weight = jax.random.normal(k5, (C, C), dtype=jnp.float32) * std
        return {'x': x, 'sources': sources, 'targets': targets, 'norm': norm, 'weight': weight}
    _L1_gnn_all = _L1_gnn_setup()
    _L1_gnn_in = {k: v for k, v in _L1_gnn_all.items() if k in ('weight',)}
    del _L1_gnn_all

    def _L1_mix_setup():
        import jax, jax.numpy as jnp
        import numpy as np
        EMB, HEADS, DEPTH, SEQ, BATCH = (256, 8, 4, 512, 4)
        DH = EMB // HEADS
        FF = 4 * EMB
        EPS = 1e-05

        def _layernorm(x, g, b):
            mu = x.mean(-1, keepdims=True)
            var = ((x - mu) ** 2).mean(-1, keepdims=True)
            return (x - mu) * jax.lax.rsqrt(var + EPS) * g + b

        def _linear_attn(x, Wq, Wk, Wv, Wo, bo):
            b, n, dm = x.shape
            split = lambda t: t.reshape(b, n, HEADS, DH).transpose(0, 2, 1, 3)
            scale = DH ** (-0.25)
            q = jax.nn.softmax(split(x @ Wq) * scale, axis=-1)
            k = jax.nn.softmax(split(x @ Wk) * scale, axis=-2)
            v = split(x @ Wv)
            context = jnp.einsum('bhnd,bhne->bhde', k, v)
            out = jnp.einsum('bhnd,bhde->bhne', q, context)
            out = out.transpose(0, 2, 1, 3).reshape(b, n, dm)
            return out @ Wo + bo

        def _forward(x, Wq, Wk, Wv, Wo, bo, ln1_g, ln1_b, W1, b1, W2, b2, ln2_g, ln2_b):
            for i in range(DEPTH):
                h = _layernorm(x, ln1_g[i], ln1_b[i])
                x = x + _linear_attn(h, Wq[i], Wk[i], Wv[i], Wo[i], bo[i])
                h = _layernorm(x, ln2_g[i], ln2_b[i])
                x = x + (jax.nn.gelu(h @ W1[i] + b1[i], approximate=False) @ W2[i] + b2[i])
            return x
        key = jax.random.key(seed)
        ks = jax.random.split(key, 8)
        w = lambda k, shape: jax.random.normal(k, shape, dtype=jnp.float32) * 0.02
        D = DEPTH
        return {'x': jax.random.normal(ks[0], (BATCH, SEQ, EMB), dtype=jnp.float32), 'Wq': w(ks[1], (D, EMB, EMB)), 'Wk': w(ks[2], (D, EMB, EMB)), 'Wv': w(ks[3], (D, EMB, EMB)), 'Wo': w(ks[4], (D, EMB, EMB)), 'bo': jnp.zeros((D, EMB), jnp.float32), 'ln1_g': jnp.ones((D, EMB), jnp.float32), 'ln1_b': jnp.zeros((D, EMB), jnp.float32), 'W1': w(ks[5], (D, EMB, FF)), 'b1': jnp.zeros((D, FF), jnp.float32), 'W2': w(ks[6], (D, FF, EMB)), 'b2': jnp.zeros((D, EMB), jnp.float32), 'ln2_g': jnp.ones((D, EMB), jnp.float32), 'ln2_b': jnp.zeros((D, EMB), jnp.float32)}
    _L1_mix_all = _L1_mix_setup()
    _L1_mix_in = {k: v for k, v in _L1_mix_all.items() if k in ('Wq', 'Wk', 'Wv', 'Wo', 'bo', 'ln1_g', 'ln1_b', 'W1', 'b1', 'W2', 'b2', 'ln2_g', 'ln2_b')}
    del _L1_mix_all

    def _L1_ffn_setup():
        import jax, jax.numpy as jnp
        import numpy as np
        E, D, H, TOP_K = (6, 256, 256, 2)
        ROUTER_H = D // 2
        key = jax.random.key(seed)
        ks = jax.random.split(key, 12)
        s = 1.0 / np.sqrt(D)
        sh = 1.0 / np.sqrt(H)
        sr = 1.0 / np.sqrt(ROUTER_H)
        return {'features': jax.random.normal(ks[0], (8, 256, D), dtype=jnp.float32), 'router_w1': jax.random.uniform(ks[1], (D, ROUTER_H), jnp.float32, -s, s), 'router_b1': jnp.zeros((ROUTER_H,), jnp.float32), 'router_w2': jax.random.uniform(ks[2], (ROUTER_H, E), jnp.float32, -sr, sr), 'router_b2': jnp.zeros((E,), jnp.float32), 'expert_w1': jax.random.uniform(ks[3], (E, D, H), jnp.float32, -s, s), 'expert_b1': jnp.zeros((E, H), jnp.float32), 'expert_w2': jax.random.uniform(ks[4], (E, H, H), jnp.float32, -sh, sh), 'expert_b2': jnp.zeros((E, H), jnp.float32), 'expert_w3': jax.random.uniform(ks[5], (E, H, D), jnp.float32, -sh, sh), 'expert_b3': jnp.zeros((E, D), jnp.float32)}
    _L1_ffn_all = _L1_ffn_setup()
    _L1_ffn_in = {k: v for k, v in _L1_ffn_all.items() if k in ('router_w1', 'router_b1', 'router_w2', 'router_b2', 'expert_w1', 'expert_b1', 'expert_w2', 'expert_b2', 'expert_w3', 'expert_b3')}
    del _L1_ffn_all
    return {'x': x, 'src': src, 'dst': dst, 'edge_weight': edge_weight, 'L0_gnn_W1': _L0_gnn_in['W1'], 'L0_gnn_b1': _L0_gnn_in['b1'], 'L0_gnn_W2': _L0_gnn_in['W2'], 'L0_gnn_b2': _L0_gnn_in['b2'], 'L0_mix_Wq': _L0_mix_in['Wq'], 'L0_mix_Wk': _L0_mix_in['Wk'], 'L0_mix_Wv': _L0_mix_in['Wv'], 'L0_mix_Wm': _L0_mix_in['Wm'], 'L0_mix_W1': _L0_mix_in['W1'], 'L0_mix_W2': _L0_mix_in['W2'], 'L0_mix_g1': _L0_mix_in['g1'], 'L0_mix_b1': _L0_mix_in['b1'], 'L0_mix_g2': _L0_mix_in['g2'], 'L0_mix_b2': _L0_mix_in['b2'], 'L0_ffn_router_w': _L0_ffn_in['router_w'], 'L0_ffn_router_b': _L0_ffn_in['router_b'], 'L0_ffn_W1': _L0_ffn_in['W1'], 'L0_ffn_b1': _L0_ffn_in['b1'], 'L0_ffn_W2': _L0_ffn_in['W2'], 'L0_ffn_b2': _L0_ffn_in['b2'], 'L1_gnn_weight': _L1_gnn_in['weight'], 'L1_mix_Wq': _L1_mix_in['Wq'], 'L1_mix_Wk': _L1_mix_in['Wk'], 'L1_mix_Wv': _L1_mix_in['Wv'], 'L1_mix_Wo': _L1_mix_in['Wo'], 'L1_mix_bo': _L1_mix_in['bo'], 'L1_mix_ln1_g': _L1_mix_in['ln1_g'], 'L1_mix_ln1_b': _L1_mix_in['ln1_b'], 'L1_mix_W1': _L1_mix_in['W1'], 'L1_mix_b1': _L1_mix_in['b1'], 'L1_mix_W2': _L1_mix_in['W2'], 'L1_mix_b2': _L1_mix_in['b2'], 'L1_mix_ln2_g': _L1_mix_in['ln2_g'], 'L1_mix_ln2_b': _L1_mix_in['ln2_b'], 'L1_ffn_router_w1': _L1_ffn_in['router_w1'], 'L1_ffn_router_b1': _L1_ffn_in['router_b1'], 'L1_ffn_router_w2': _L1_ffn_in['router_w2'], 'L1_ffn_router_b2': _L1_ffn_in['router_b2'], 'L1_ffn_expert_w1': _L1_ffn_in['expert_w1'], 'L1_ffn_expert_b1': _L1_ffn_in['expert_b1'], 'L1_ffn_expert_w2': _L1_ffn_in['expert_w2'], 'L1_ffn_expert_b2': _L1_ffn_in['expert_b2'], 'L1_ffn_expert_w3': _L1_ffn_in['expert_w3'], 'L1_ffn_expert_b3': _L1_ffn_in['expert_b3']}

def reference(x, src, dst, edge_weight, L0_gnn_W1, L0_gnn_b1, L0_gnn_W2, L0_gnn_b2, L0_mix_Wq, L0_mix_Wk, L0_mix_Wv, L0_mix_Wm, L0_mix_W1, L0_mix_W2, L0_mix_g1, L0_mix_b1, L0_mix_g2, L0_mix_b2, L0_ffn_router_w, L0_ffn_router_b, L0_ffn_W1, L0_ffn_b1, L0_ffn_W2, L0_ffn_b2, L1_gnn_weight, L1_mix_Wq, L1_mix_Wk, L1_mix_Wv, L1_mix_Wo, L1_mix_bo, L1_mix_ln1_g, L1_mix_ln1_b, L1_mix_W1, L1_mix_b1, L1_mix_W2, L1_mix_b2, L1_mix_ln2_g, L1_mix_ln2_b, L1_ffn_router_w1, L1_ffn_router_b1, L1_ffn_router_w2, L1_ffn_router_b2, L1_ffn_expert_w1, L1_ffn_expert_b1, L1_ffn_expert_w2, L1_ffn_expert_b2, L1_ffn_expert_w3, L1_ffn_expert_b3):
    import jax
    import jax.numpy as jnp

    def _L0_gnn_ref(x, edge_index, edge_weight, W1, b1, W2, b2):
        import jax, jax.numpy as jnp
        import numpy as np
        N, D, E = (6250, 256, 312500)
        H = 2 * D
        EPS = 0.0
        row, col = (edge_index[0], edge_index[1])
        messages = x[col] * edge_weight[:, None]
        agg = jax.ops.segment_sum(messages, row, num_segments=N)
        h = (1.0 + EPS) * x + agg
        h = jax.nn.relu(h @ W1 + b1)
        out = h @ W2 + b2
        return out

    def _L0_mix_ref(x, Wq, Wk, Wv, Wm, W1, W2, g1, b1, g2, b2):
        import jax, jax.numpy as jnp
        import numpy as np
        NHEAD = 8
        ATT_EPS = 1e-06
        LN_EPS = 1e-05

        def _layernorm(x, g, b):
            mu = jnp.mean(x, axis=-1, keepdims=True)
            var = jnp.mean(jnp.square(x - mu), axis=-1, keepdims=True)
            return (x - mu) * jax.lax.rsqrt(var + LN_EPS) * g + b
        N, L, C = x.shape
        H = NHEAD
        D = C // H
        q = (x @ Wq).reshape(N, L, H, D)
        k = (x @ Wk).reshape(N, L, H, D)
        v = (x @ Wv).reshape(N, L, H, D)
        Q = jax.nn.elu(q) + 1.0
        K = jax.nn.elu(k) + 1.0
        v = v / L
        KV = jnp.einsum('nshd,nshv->nhdv', K, v)
        Z = 1.0 / (jnp.einsum('nlhd,nhd->nlh', Q, K.sum(axis=1)) + ATT_EPS)
        msg = jnp.einsum('nlhd,nhdv,nlh->nlhv', Q, KV, Z) * L
        msg = msg.reshape(N, L, C) @ Wm
        msg = _layernorm(msg, g1, b1)
        h = jnp.concatenate([x, msg], axis=-1) @ W1
        h = jax.nn.relu(h) @ W2
        msg = _layernorm(h, g2, b2)
        return x + msg

    def _L0_ffn_ref(x, router_w, router_b, W1, b1, W2, b2):
        import jax, jax.numpy as jnp
        import numpy as np
        B, K, D = (512, 16, 256)
        E = 32
        H = int(D * 0.25)
        xf = x.reshape(-1, D)
        logits = xf @ router_w.T + router_b
        idx = jnp.argmax(logits, axis=-1)
        w1t = jnp.take(W1, idx, axis=0)
        h = jnp.einsum('nd,ndh->nh', xf, w1t) + jnp.take(b1, idx, axis=0)
        h = jax.nn.relu(h)
        w2t = jnp.take(W2, idx, axis=0)
        out = jnp.einsum('nh,nhd->nd', h, w2t) + jnp.take(b2, idx, axis=0)
        out = jax.nn.relu(out)
        return out.reshape(x.shape)

    def _L1_gnn_ref(x, sources, targets, norm, weight):
        import jax, jax.numpy as jnp
        import numpy as np
        N = 12500
        E = 37500
        C = 256
        agg = x.at[targets].add(x[sources])
        h = norm * agg
        return h @ weight

    def _L1_mix_ref(x, Wq, Wk, Wv, Wo, bo, ln1_g, ln1_b, W1, b1, W2, b2, ln2_g, ln2_b):
        import jax, jax.numpy as jnp
        import numpy as np
        EMB, HEADS, DEPTH, SEQ, BATCH = (256, 8, 4, 512, 4)
        DH = EMB // HEADS
        FF = 4 * EMB
        EPS = 1e-05

        def _layernorm(x, g, b):
            mu = x.mean(-1, keepdims=True)
            var = ((x - mu) ** 2).mean(-1, keepdims=True)
            return (x - mu) * jax.lax.rsqrt(var + EPS) * g + b

        def _linear_attn(x, Wq, Wk, Wv, Wo, bo):
            b, n, dm = x.shape
            split = lambda t: t.reshape(b, n, HEADS, DH).transpose(0, 2, 1, 3)
            scale = DH ** (-0.25)
            q = jax.nn.softmax(split(x @ Wq) * scale, axis=-1)
            k = jax.nn.softmax(split(x @ Wk) * scale, axis=-2)
            v = split(x @ Wv)
            context = jnp.einsum('bhnd,bhne->bhde', k, v)
            out = jnp.einsum('bhnd,bhde->bhne', q, context)
            out = out.transpose(0, 2, 1, 3).reshape(b, n, dm)
            return out @ Wo + bo

        def _forward(x, Wq, Wk, Wv, Wo, bo, ln1_g, ln1_b, W1, b1, W2, b2, ln2_g, ln2_b):
            for i in range(DEPTH):
                h = _layernorm(x, ln1_g[i], ln1_b[i])
                x = x + _linear_attn(h, Wq[i], Wk[i], Wv[i], Wo[i], bo[i])
                h = _layernorm(x, ln2_g[i], ln2_b[i])
                x = x + (jax.nn.gelu(h @ W1[i] + b1[i], approximate=False) @ W2[i] + b2[i])
            return x
        return _forward(x, Wq, Wk, Wv, Wo, bo, ln1_g, ln1_b, W1, b1, W2, b2, ln2_g, ln2_b)

    def _L1_ffn_ref(features, router_w1, router_b1, router_w2, router_b2, expert_w1, expert_b1, expert_w2, expert_b2, expert_w3, expert_b3):
        import jax, jax.numpy as jnp
        import numpy as np
        E, D, H, TOP_K = (6, 256, 256, 2)
        ROUTER_H = D // 2
        rh = jax.nn.relu(features @ router_w1 + router_b1)
        expert_logits = jax.nn.softmax(rh @ router_w2 + router_b2, axis=-1)
        top_w, top_i = jax.lax.top_k(expert_logits, TOP_K)
        routing_weights = jax.nn.softmax(top_w, axis=-1)
        h1 = jax.nn.relu(jnp.einsum('bsd,edh->bseh', features, expert_w1) + expert_b1)
        h2 = jax.nn.relu(jnp.einsum('bseh,ehf->bsef', h1, expert_w2) + expert_b2)
        expert_out = jnp.einsum('bsef,efo->bseo', h2, expert_w3) + expert_b3
        sel = jnp.take_along_axis(expert_out, top_i[:, :, :, None], axis=2)
        combined = jnp.sum(sel * routing_weights[..., None], axis=2)
        return combined
    edge_index = jnp.stack([src, dst])
    deg = jnp.maximum(jax.ops.segment_sum(jnp.ones(dst.shape, jnp.float32), dst, num_segments=6250), 1.0)
    deg_isqrt = deg ** (-0.5)
    xn = _layernorm(x, axis=-1)
    x = x + _L0_gnn_ref(xn, edge_index, edge_weight, L0_gnn_W1, L0_gnn_b1, L0_gnn_W2, L0_gnn_b2) + _L0_mix_ref(xn[None], L0_mix_Wq, L0_mix_Wk, L0_mix_Wv, L0_mix_Wm, L0_mix_W1, L0_mix_W2, L0_mix_g1, L0_mix_b1, L0_mix_g2, L0_mix_b2)[0]
    x = x + _L0_ffn_ref(_layernorm(x, axis=-1)[None], L0_ffn_router_w, L0_ffn_router_b, L0_ffn_W1, L0_ffn_b1, L0_ffn_W2, L0_ffn_b2)[0]
    xn = _layernorm(x, axis=-1)
    x = x + _L1_gnn_ref(xn, src, dst, deg_isqrt[:, None], L1_gnn_weight) + _L1_mix_ref(xn[None], L1_mix_Wq, L1_mix_Wk, L1_mix_Wv, L1_mix_Wo, L1_mix_bo, L1_mix_ln1_g, L1_mix_ln1_b, L1_mix_W1, L1_mix_b1, L1_mix_W2, L1_mix_b2, L1_mix_ln2_g, L1_mix_ln2_b)[0]
    x = x + _L1_ffn_ref(_layernorm(x, axis=-1)[None], L1_ffn_router_w1, L1_ffn_router_b1, L1_ffn_router_w2, L1_ffn_router_b2, L1_ffn_expert_w1, L1_ffn_expert_b1, L1_ffn_expert_w2, L1_ffn_expert_b2, L1_ffn_expert_w3, L1_ffn_expert_b3)[0]
    return x

_drawn_inputs = setup_inputs


def setup_inputs(seed=0):
    import zlib

    import numpy as np

    out = dict(_drawn_inputs(seed))
    spreads = {'L0_mix_g1': (1.0, 0.2),
     'L0_mix_b1': (0.0, 0.1),
     'L0_mix_g2': (1.0, 0.2),
     'L0_mix_b2': (0.0, 0.1),
     'L1_mix_bo': (0.0, 0.1),
     'L1_mix_ln1_g': (1.0, 0.6),
     'L1_mix_ln1_b': (0.0, 0.8),
     'L1_mix_b1': (0.0, 0.416),
     'L1_mix_b2': (0.0, 0.1),
     'L1_mix_ln2_g': (1.0, 0.6),
     'L1_mix_ln2_b': (0.0, 0.8),
     'L1_ffn_router_b1': (0.0, 0.686),
     'L1_ffn_router_b2': (0.0, 0.765),
     'L1_ffn_expert_b1': (0.0, 0.8),
     'L1_ffn_expert_b2': (0.0, 0.8),
     'L1_ffn_expert_b3': (0.0, 0.443)}
    factors = {'L0_gnn_b1': 6.2,
     'L0_gnn_b2': 3.308,
     'L0_ffn_router_b': 2.999,
     'L0_ffn_b1': 8.0,
     'L0_ffn_b2': 5.604,
     'L1_mix_Wq': 8.0,
     'L1_mix_Wk': 23.387,
     'L1_ffn_expert_w1': 4.193,
     'L1_ffn_expert_w2': 3.737,
     'L1_ffn_expert_w3': 2.871}
    for name, (base, spread) in spreads.items():
        noise = np.random.default_rng([zlib.crc32(name.encode()), seed]).standard_normal(out[name].shape)
        drawn = base * np.exp(spread * noise) if base else spread * noise
        out[name] = jnp.asarray(drawn.astype(out[name].dtype))
    for name, factor in factors.items():
        out[name] = (out[name] * factor).astype(out[name].dtype)
    return out
```

```python
from contextlib import ExitStack

import concourse.bass as bass
from concourse import mybir
from concourse.alu_op_type import AluOpType as ALU

F32 = mybir.dt.float32
BF16 = mybir.dt.bfloat16
I32 = mybir.dt.int32
U32 = mybir.dt.uint32
ACT = mybir.ActivationFunctionType
AX = mybir.AxisListType

N, D, E = 6250, 256, 100000
T = 125
NT = N // T
CH = 2 * T
NC = N // CH
NP = (NC + 1) // 2
EC = E // T
GR = 256
NG = (E + NT * (GR - 1)) // GR
NS = 2 * NG
HEADS, DH = 8, 32
LAYERS = 4
NEXP, HEXP = 32, 64
NEXP1 = 6
EPS = 1e-5
ATT_EPS = 1e-6
SCALE = DH ** -0.25
LOWEST = -3.0e38
ROUND = 12582912.0
GUESS = 0x5F3759DF
MASKED = 1e30
RING = 8
assert T * EC == E and NC % 2 == 1 and NS % (2 * RING) == 0 and EC % (2 * RING) == 0

RSQRT = ["var", "bits", "half", "guess"] + [f"newton{n}{x}" for n in range(3) for x in "abc"]
LN = ["stats", "mean"] + RSQRT
KINDS = {
    "A0": dict(pe=["zT", "k", "v", "q", "ctx"], act=["zT", "v", "kexp", "qexp"],
               dve=LN + ["z", "kmin", "qmin", "k", "q", "ctx"]),
    "B0": dict(pe=["qT", "msg", "mT", "h0", "h1", "out"], act=["qT", "mT", "h0", "h1"],
               dve=["prod", "den", "deneps", "denrec", "q"] + LN + ["m"] + ["o" + x for x in LN]
               + ["oz", "og", "ox", "or", "r"]),
    "C0a": dict(pe=["hT", "h0", "h1", "out"], act=["hT", "h0", "h1"], dve=["h", "x1"]),
    "C0b": dict(pe=["zT", "logit", "oneT", "h0"] + sum([[f"h{p}", f"o{p - 1}"] for p in range(1, 8)], [])
                + ["out"],
                act=["zT"] + [f"h{p}" for p in range(8)] + ["xm"],
                dve=LN + ["z", "logit", "max", "arg", "argf", "one", "oneT", "mask", "x2"]
                + ["n" + x for x in LN] + ["xn"]),
    "A1": dict(pe=["zT", "k", "v", "kT", "q", "ctx", "qT"], act=["zT", "v", "drop", "kexp", "qexp", "qT"],
               dve=LN + ["z", "kmax", "pairmax", "runmax", "negmax", "drop", "keep", "kT", "qmax", "qsub",
                         "qsum", "qrec", "q", "ctx"]),
    "B1": dict(pe=["att", "zT", "h0", "h1", "h2", "o0", "h3", "o1", "o2", "out"],
               act=["zT", "h0", "h1", "h2", "h3"],
               dve=["att", "bo"] + LN + ["z", "out", "b2"]),
    "C1a": dict(pe=["hT", "out"], act=["hT"], dve=["h", "hs", "xa", "x3"]),
    "C1b": dict(pe=["zT", "rh", "logit", "gT", "yb", "a0", "b0"]
                + sum([[f"a{e}", f"o{e - 1}", f"b{e}"] for e in range(1, NEXP1)], []) + ["out"],
                act=["zT", "rh", "pexp", "gexp", "gT"] + sum([[f"a{e}", f"b{e}"] for e in range(NEXP1)], []),
                dve=LN + ["z", "logit", "lmax", "lsub", "lsum", "lrec", "p", "max", "arg", "argf", "gdif",
                          "gsum", "g1", "g2", "one", "gate", "yb"] + [f"y{e}" for e in range(NEXP1)]),
}
PHASES = ["A0", "B0", "C0a", "C0b"] + [x for n in range(LAYERS) for x in (f"A1.{n}", f"B1.{n}")] + ["C1a", "C1b"]


TURNS = {f"{x}1.{n}": t for n in range(1, LAYERS) for x, t in (("A", 1), ("B", 2))}
TURNS_BEFORE, _turns = {}, 0
for _phase in TURNS:
    TURNS_BEFORE[_phase] = _turns
    _turns += TURNS[_phase] * (NP - 1)
LAST_TURNS = NS // RING - _turns
GROUPS = RING // 2


def turns(phase, i):
    if phase not in TURNS:
        return 0, 0
    if isinstance(i, int) and i == NP - 1:
        return _turns, LAST_TURNS if phase == f"B1.{LAYERS - 1}" else 0
    return i * TURNS[phase] + TURNS_BEFORE[phase], TURNS[phase]


def kind(phase):
    return phase.split(".")[0]


class Stages:

    def __init__(self, sem, engine):
        self.sem, self.base, self.names, self.next = sem, {}, {}, 0
        at = 0
        for phase in PHASES:
            self.names[phase] = KINDS[kind(phase)][engine]
            self.base[phase] = at
            at += 2 * len(self.names[phase]) * NP
        self.base["end"] = at

    def done(self, phase, stage, i, s=1):
        names = self.names[phase]
        return self.sem, 2 * len(names) * i + (self.base[phase] + 2 * names.index(stage) + s + 1)

    def add(self, phase, stage, slots, s=None):
        names = self.names[phase]
        assert names[self.next // 2] == stage and (self.next % 2 if s else not self.next % 2), stage
        n = 2 if s is None else 3 - len(slots)
        self.next = (self.next + n) % (2 * len(names))
        return self.sem, n

    def all(self, phase):
        return self.sem, self.base[phase]


class Transfers:

    def __init__(self, sems, phases):
        self.sems, self.phases = sems, phases

    def done(self, phase, i, s):
        before = self.phases.index(phase) * (NP - s)
        return self.sems[s], 16 * i + 16 * (before + 1)

    def all(self, phase):
        n = sum(PHASES.index(p) < PHASES.index(phase) for p in self.phases)
        return [(self.sems[s], 16 * n * (NP - s)) for s in range(2)]


def pairs(engine, body):
    body(0, (0, 1))
    with engine.Fori(1, NP - 1) as i:
        body(i, (0, 1))
    body(NP - 1, (0,))


def pairs_ahead(engine, load, store):
    load(0, (0, 1))
    load(1, (0, 1))
    store(0, (0, 1))
    with engine.Fori(1, NP - 2) as i:
        load(i + 1, (0, 1))
        store(i, (0, 1))
    load(NP - 1, (0,))
    store(NP - 2, (0, 1))
    store(NP - 1, (0,))


def first(i):
    return isinstance(i, int) and i == 0


def build(nc, a, out):
    ctx = ExitStack()
    with ctx:
        def sb(name, shape, dt=F32):
            return ctx.enter_context(nc.sbuf_tensor("sb_" + name, shape, dt))

        def sem(name):
            return ctx.enter_context(nc.semaphore(name))

        def dram(name, shape, dt=F32):
            return nc.dram_tensor("scratch_" + name, shape, dt).ap()

        xn0_d, r_d, x2_d, xn1_d, q0_d = (dram(n, [N, D]) for n in ("xn0", "r", "x2", "xn1", "q0"))
        xT_d, qT_d = (dram(n, [NC, 128, 2 * CH]) for n in ("xT", "qT"))
        sorted_d = [dram(f"sorted{e}", [128 * NS, 3]) for e in range(2)]
        rec1_d, pos1_d = dram("rec1", [T, EC * 3]), dram("pos1", [T, EC], U32)

        def tiles(x):
            return x.rearrange("(t p) n -> p t n", p=T)

        xm_all = sb("XM", [128, NT * D])
        agg_all = sb("AGG", [128, NT * (D + 1)])
        XM = xm_all[0:T, :].rearrange("p (t n) -> p t n", n=D)
        AGG = agg_all[0:T, :].rearrange("p (t n) -> p t n", n=D + 1)
        work = {n: sb("work_" + n, [128, 2, 512]) for n in ("XC", "ZT", "QT", "KT", "TM", "FT", "QF")}
        VT = sb("VT", [T, 2, 2, 2, 129])
        HT = sb("HT", [128, 2, 8, CH])
        W0 = sb("W0", [128, 2048])
        W1 = sb("W1", [128, 4096])
        rows = sb("rows", [128, RING, D + 1])
        onehot = work["TM"][:, :, :].rearrange("p s n -> p (s n)")[:, 0:RING * T].rearrange("p (u n) -> p u n", n=T)
        srec = sb("srec", [128, NS, 3])
        gblk = sb("gblk", [1, 2, NG], I32)
        ring_idx = sb("ring_idx", [128, 2, RING], U32)
        ring_rec = sb("ring_rec", [T, 2, RING * 3])
        ident = sb("ident", [128, 128])
        ones = sb("ones", [128, 128])
        lower = sb("lower", [128, 128])
        blocks = sb("blocks", [128, 128])
        iota_t = sb("iota_t", [128, T])
        iota_b = sb("iota_b", [T, NT])
        iota32 = sb("iota32", [T, NEXP])
        CTX = sb("CTX", [128, 2, 129])
        KR = sb("KR", [128, 2, 1])
        MM = sb("MM", [128, 2, D])
        rowA, rowB = sb("rowA", [T, D]), sb("rowB", [T, D])
        rowR, rowS = sb("rowR", [T, NEXP]), sb("rowS", [T, NEXP1])
        STAT, MV = sb("STAT", [T, 2, 2, 6]), sb("MV", [T, 2, 2, 2])
        RV, RY, RT = (sb(n, [T, 2, 2]) for n in ("RV", "RY", "RT"))
        DN = sb("DN", [T, 2, 16])
        KM = sb("KM", [128, 2, 2])
        NM, NEG, AL, RUN = (sb(n, [128, 2]) for n in ("NM", "NEG", "AL", "RUN"))
        LG, OH = sb("LG", [T, 2, 2, NEXP]), sb("OH", [T, 2, 2, NEXP])
        MX, IXF = sb("MX", [T, 2, 2, 8]), sb("IXF", [T, 2, 2, 8])
        IX = sb("IX", [T, 2, 2, 8], U32)
        LM, GD, GA, GB = (sb(n, [T, 2, 2]) for n in ("LM", "GD", "GA", "GB"))
        DG, DY, DT = (sb(n, [T, NT]) for n in ("DG", "DY", "DT"))
        zero = sb("zero", [T, 1])
        grT, gendT = sb("grT", [NT, 1]), sb("gendT", [NT, 1])

        vectors = {"g1": "L0_mix_g1", "b1": "L0_mix_b1", "gnn_b1": "L0_gnn_b1", "exp_b1": "L0_ffn_b1",
                   "ln1_g": "L1_mix_ln1_g", "ln1_b": "L1_mix_ln1_b", "ln2_g": "L1_mix_ln2_g",
                   "ln2_b": "L1_mix_ln2_b", "up_b": "L1_mix_b1", "rh_b": "L1_ffn_router_b1",
                   "exp1_b1": "L1_ffn_expert_b1", "exp1_b2": "L1_ffn_expert_b2"}
        col_at, at = {}, 0
        for name, source in vectors.items():
            col_at[name] = at
            size = 1
            for d in a[source].shape:
                size *= d
            at += size // 128
        cols = sb("cols", [128, at])
        n_cols = at

        def col(name, n):
            return cols[:, col_at[name] + n:col_at[name] + n + 1]

        def tok(b, s):
            return b[0:T, s, :].rearrange("p (t n) -> p t n", t=2)

        def feat(b, s):
            return b[:, s, 0:2 * CH].rearrange("p (k n) -> p k n", k=2)

        XC, ZT, QT, KT, TM = ([tok(work[n], s) for s in range(2)] for n in ("XC", "ZT", "QT", "KT", "TM"))
        FT, QF, PF = ([feat(work[n], s) for s in range(2)] for n in ("FT", "QF", "XC"))

        def heads(x):
            return x.rearrange("p t (h d) -> p (t h) d", d=DH)

        def per_head(s):
            return DN[:, s, :].rearrange("p (h u) -> p h u", u=1).to_broadcast([T, 2 * HEADS, DH])

        def both(row):
            return row.rearrange("p (u n) -> p u n", u=1).to_broadcast([T, 2, D])

        bank = [ctx.enter_context(nc.psum_tensor(f"bank{n}", [128, 512], F32)) for n in range(8)]
        PA, PB, PC = ([bank[3 * s + n] for s in range(2)] for n in range(3))
        PSUMS = bank[6:8]

        def ptok(b):
            return b[0:T, :].rearrange("p (t n) -> p t n", t=2)

        def pfeat(b):
            return b[:, 0:2 * CH].rearrange("p (k n) -> p k n", k=2)

        def part(region, at, k, n):
            return region[:, at:at + k * n].rearrange("p (k n) -> p k n", k=k)

        def byk(w):
            return w.rearrange("(k p) n -> p k n", p=128)

        wq, wk, wv, wo = (part(W0, 512 * n, 2, D) for n in range(4))
        w0_gnn1, w0_gnn2 = part(W0, 0, 2, 512), part(W0, 1024, 4, D)
        w1_gnn = part(W0, 0, 2, D)
        w0_m, w0_mix1, w0_mix2 = part(W1, 0, 2, D), part(W1, 512, 4, 512), part(W1, 2560, 4, D)
        w1_up, w1_down = part(W1, 0, 2, 1024), part(W1, 2048, 8, D)
        w0_up, w0_down = part(agg_all, 0, 2, NEXP * HEXP), part(agg_all, 4096, 16, D)
        KSB, rowC = W1[0:T, 3584:3840], W1[0:T, 3840:4096]
        KD, CN, CNT = (HT[:, 0, 2 * n:2 * n + 2, 0:128] for n in range(3))
        select = W1[0:NEXP, 0:1024].bitcast(BF16)
        OHT = W1[0:NEXP, 1024:1024 + 2 * CH].rearrange("p (s n) -> p s n", s=2)
        OHM = W1[0:NEXP, 1536:1536 + CH].bitcast(BF16).rearrange("p (s n) -> p s n", s=2)
        bexp0 = W1[0:NEXP, 2048:2048 + D]
        bexp1 = W1[0:NEXP1, 0:D]
        GT = W1[0:8, 256:256 + 2 * CH].rearrange("p (s n) -> p s n", s=2)
        P8, G1, G2 = (W1[0:T, at:at + 32].rearrange("p (s t e) -> p s t e", s=2, t=2) for at in (768, 800, 832))
        vector_rows, router_rows = HT[0:n_cols, 1, 0, 0:128], HT[0:NEXP, 1, 2:4, 0:128]
        w0_router = sb("w0_router", [128, 2, NEXP])
        w1_exp = [[part(agg_all, 512 * (NEXP1 * m + e), 2, D) for e in range(NEXP1)] for m in range(3)]
        w1_rh, w1_router = part(agg_all, 512 * 3 * NEXP1, 2, 128), part(agg_all, 512 * 3 * NEXP1 + 256, 1, NEXP1)

        def xs(n, w=1):
            return xm_all[0:T, n * EC:(n + w) * EC]

        src_i, dst_i, ew = xs(0).bitcast(I32), xs(1).bitcast(I32), xs(2)
        pos = [xs(3).bitcast(U32), xs(7).bitcast(U32)]
        rec = [xs(4, 3), xs(8, 3)]
        keyf, blk, is_b, scan, rank, start, lane, tmp = (agg_all[0:T, n * EC:(n + 1) * EC] for n in range(8))
        iota_g = agg_all[0:NT, 8 * EC:8 * EC + NG]
        gcmp = agg_all[0:NT, 8 * EC + NG:8 * EC + 2 * NG]
        tot, gr, gend, base = (agg_all[0:T, n:n + NT] for n in range(8 * EC + 2 * NG, 8 * EC + 2 * NG + 4 * NT, NT))
        pos1_again = agg_all[0:T, 8192:8192 + EC].bitcast(U32)
        rec1_again = agg_all[0:T, 8192 + EC:8192 + 4 * EC]

        pe_done = Stages(sem("psum_filled"), "pe")
        act_done = Stages(sem("act_stage_done"), "act")
        dve_done = Stages(sem("dve_stage_done"), "dve")

        def transfers(name, phases):
            return Transfers([sem(f"{name}_{s}") for s in range(2)], phases)

        x_loaded = transfers("x_loaded", ["A0", "B0", "C0a", "C1a"])
        z_loaded = transfers("z_loaded", ["B0", "C0a", "C1a"])
        q_loaded = transfers("q_loaded", ["B0"] + [f"B1.{n}" for n in range(LAYERS)])
        f_loaded = transfers("f_loaded", ["B0"])
        q_stored = transfers("q_stored", ["A0"] + [f"A1.{n}" for n in range(LAYERS)])
        z_stored = transfers("z_stored", ["A0", "C0b"])
        f_stored = transfers("f_stored", ["A0"])
        x_stored = transfers("x_stored", ["C0b"])
        k_stored = transfers("k_stored", ["B0", "C1b"])
        ALL_TRANSFERS = [x_loaded, z_loaded, q_loaded, f_loaded, q_stored, z_stored, f_stored, x_stored, k_stored]

        weights_loaded = {p: sem("weights_" + p.replace(".", "_")) for p in PHASES}
        weight_loads = {}
        consts_loaded = sem("consts_loaded")
        consts_made = sem("consts_made")
        consts_turned = sem("consts_turned")
        edges_loaded = sem("edges_loaded")
        blanked = sem("blanked")
        context_step = sem("context_step")
        sort_step = sem("sort_step")
        sort_sums = sem("sort_sums")
        spilled = sem("spilled")
        unspilled = sem("unspilled")
        ring_copied = sem("ring_copied")
        scattered = [sem(f"scattered_{h}") for h in range(2)]
        srec_loaded = sem("srec_loaded")
        gathered = [sem(f"gathered_{q}") for q in range(RING)]
        row_free = sem("row_free")
        onehot_made = sem("onehot_made")
        group_added = sem("group_added")
        agg_zeroed = sem("agg_zeroed")
        degree_step = sem("degree_step")

        def wait(engine, mark):
            engine.wait_ge(*mark)

        def hold(engine):
            engine.nop(nofuse=True)

        def enter(engine, phase):
            for stages in (pe_done, act_done, dve_done):
                if phase != "A0":
                    wait(engine, stages.all(phase))
            for t in ALL_TRANSFERS:
                for mark in t.all(phase):
                    if mark[1]:
                        wait(engine, mark)

        CONTEXTS = ["A0"] + [f"A1.{n}" for n in range(LAYERS)]
        CONTEXT_STEPS = ["scaled", "masked", "turned", "turned_out", "times_w", "ready", "cleared"]

        def context(phase, step):
            return context_step, len(CONTEXT_STEPS) * CONTEXTS.index(phase) + CONTEXT_STEPS.index(step) + 1

        SORT_STEPS = 9 + 4 * NT + 7 + 2 * NT + 6 + 3

        block = ctx.enter_context(nc.Block())

        @block.sync
        def _(sp):
            def load(phase, *moves):
                for dst, source in moves:
                    sp.dma_start(dst, source).then_inc(weights_loaded[phase], 16)
                weight_loads[phase] = 16 * len(moves)

            def row(v):
                return v.rearrange("(u n) -> u n", u=1).to_broadcast([T, v.shape[0]])

            def spread(x):
                return x.rearrange("(p c) -> p c", p=T)

            for dst, source in ((src_i, a["src"]), (dst_i, a["dst"]), (ew, a["edge_weight"])):
                sp.dma_start(dst, spread(source)).then_inc(edges_loaded, 16)
            load("A0", (wk, byk(a["L0_mix_Wk"])), (wv, byk(a["L0_mix_Wv"])), (wq, byk(a["L0_mix_Wq"])))
            for name, source in vectors.items():
                v = a[source]
                if len(v.shape) == 2:
                    v = v.rearrange("l n -> (l n)")
                n = v.shape[0] // 128
                sp.dma_start(vector_rows[col_at[name]:col_at[name] + n, :], v.rearrange("(k p) -> k p", p=128))\
                    .then_inc(consts_loaded, 16)
            sp.dma_start(rowR[:], row(a["L0_ffn_router_b"])).then_inc(consts_loaded, 16)
            sp.dma_start(rowS[:], row(a["L1_ffn_router_b2"])).then_inc(consts_loaded, 16)
            sp.dma_start(router_rows, a["L0_ffn_router_w"].rearrange("e (k p) -> e k p", k=2))\
                .then_inc(consts_loaded, 16)

            def load_a0(i, slots):
                for s in slots:
                    if not first(i):
                        wait(sp, dve_done.done("A0", "z", i - 1, s))
                    sp.dma_start(XC[s], tiles(a["x"])[:, bass.ds(4 * i + 2 * s, 2), :])\
                        .then_inc(x_loaded.sems[s], 16)

            def store_a0(i, slots):
                for s in slots:
                    wait(sp, dve_done.done("A0", "z", i, s))
                    sp.dma_start(tiles(xn0_d)[:, bass.ds(4 * i + 2 * s, 2), :], ZT[s])\
                        .then_inc(z_stored.sems[s], 16)
                for s in slots:
                    wait(sp, act_done.done("A0", "zT", i, s))
                    sp.dma_start(xT_d[bass.ds(2 * i + s, 1), :, :].rearrange("u p (k n) -> p (u k) n", k=2), FT[s])\
                        .then_inc(f_stored.sems[s], 16)
                for s in slots:
                    wait(sp, dve_done.done("A0", "q", i, s))
                    sp.dma_start(tiles(q0_d)[:, bass.ds(4 * i + 2 * s, 2), :], QT[s])\
                        .then_inc(q_stored.sems[s], 16)

            load("B0", (w0_m, byk(a["L0_mix_Wm"])), (w0_mix1, byk(a["L0_mix_W1"])),
                 (w0_mix2, byk(a["L0_mix_W2"])), (rowA[:], row(a["L0_mix_g2"])),
                 (rowB[:], row(a["L0_mix_b2"])), (rowC, row(a["L0_gnn_b2"])))
            pairs_ahead(sp, load_a0, store_a0)

            enter(sp, "B0")
            load("C0a", (w0_gnn1, byk(a["L0_gnn_W1"])), (w0_gnn2, byk(a["L0_gnn_W2"])))

            def load_b0(i, slots):
                for s in slots:
                    if not first(i):
                        wait(sp, pe_done.done("B0", "qT", i - 1, s))
                    sp.dma_start(QT[s], tiles(q0_d)[:, bass.ds(4 * i + 2 * s, 2), :])\
                        .then_inc(q_loaded.sems[s], 16)
                for s in slots:
                    if not first(i):
                        wait(sp, pe_done.done("B0", "h1", i - 1, s))
                    sp.dma_start(FT[s], xT_d[bass.ds(2 * i + s, 1), :, :].rearrange("u p (k n) -> p (u k) n", k=2))\
                        .then_inc(f_loaded.sems[s], 16)
                for s in slots:
                    if not first(i):
                        wait(sp, dve_done.done("B0", "r", i - 1, s))
                    sp.dma_start(ZT[s], tiles(xn0_d)[:, bass.ds(4 * i + 2 * s, 2), :])\
                        .then_inc(z_loaded.sems[s], 16)
                    sp.dma_start(XC[s], tiles(a["x"])[:, bass.ds(4 * i + 2 * s, 2), :])\
                        .then_inc(x_loaded.sems[s], 16)

            def store_b0(i, slots):
                for s in slots:
                    wait(sp, dve_done.done("B0", "r", i, s))
                    sp.dma_start(tiles(r_d)[:, bass.ds(4 * i + 2 * s, 2), :], KT[s])\
                        .then_inc(k_stored.sems[s], 16)

            pairs_ahead(sp, load_b0, store_b0)

            wait(sp, (sort_step, 2 * SORT_STEPS))
            sp.dma_start(rec1_d, rec[1]).then_inc(spilled, 16)
            sp.dma_start(pos1_d, pos[1]).then_inc(spilled, 16)

            def load_sorted(e):
                for h in range(2):
                    wait(sp, (scattered[h], (e + 1) * 16 * EC // 2))
                sp.dma_start(srec[:], sorted_d[e].rearrange("(p t) c -> p t c", p=128)).then_inc(srec_loaded, 16)

            load_sorted(0)

            enter(sp, "C0a")

            def load_c0a(i, slots):
                for s in slots:
                    if not first(i):
                        wait(sp, pe_done.done("C0a", "hT", i - 1, s))
                    sp.dma_start(ZT[s], tiles(xn0_d)[:, bass.ds(4 * i + 2 * s, 2), :])\
                        .then_inc(z_loaded.sems[s], 16)
                    if not first(i):
                        wait(sp, dve_done.done("C0a", "x1", i - 1, s))
                    sp.dma_start(XC[s], tiles(r_d)[:, bass.ds(4 * i + 2 * s, 2), :])\
                        .then_inc(x_loaded.sems[s], 16)

            pairs(sp, load_c0a)

            enter(sp, "C0b")
            exp_up = a["L0_ffn_W1"].rearrange("e (k p) h -> p k e h", p=128)
            load("C0b", *[(w0_up[:, k, :].rearrange("p (e h) -> p e h", e=NEXP), exp_up[:, k]) for k in range(2)],
                 (w0_down, byk(a["L0_ffn_W2"].rearrange("e h d -> (e h) d"))), (bexp0, a["L0_ffn_b2"]))
            wait(sp, (spilled, 32))
            sp.dma_start(pos1_again, pos1_d).then_inc(unspilled, 16)
            sp.dma_start(rec1_again, rec1_d).then_inc(unspilled, 16)

            def load_l1(n):
                load(f"A1.{n}", *[(dst, byk(a[f"L1_mix_W{x}"][n])) for dst, x in
                                  ((wk, "k"), (wv, "v"), (wq, "q"), (wo, "o"))])

            load_l1(0)

            def store_c0b(i, slots):
                for s in slots:
                    wait(sp, dve_done.done("C0b", "x2", i, s))
                    sp.dma_start(tiles(x2_d)[:, bass.ds(4 * i + 2 * s, 2), :], XC[s])\
                        .then_inc(x_stored.sems[s], 16)
                for s in slots:
                    wait(sp, dve_done.done("C0b", "xn", i, s))
                    sp.dma_start(tiles(xn1_d)[:, bass.ds(4 * i + 2 * s, 2), :], ZT[s])\
                        .then_inc(z_stored.sems[s], 16)

            pairs(sp, store_c0b)

            for n in range(LAYERS):
                enter(sp, f"A1.{n}")
                load(f"B1.{n}", (w1_up, byk(a["L1_mix_W1"][n])), (w1_down, byk(a["L1_mix_W2"][n])),
                     (rowA[:], row(a["L1_mix_bo"][n])), (rowB[:], row(a["L1_mix_b2"][n])))

                def store_a1(i, slots, phase=f"A1.{n}"):
                    for s in slots:
                        wait(sp, act_done.done(phase, "qT", i, s))
                        sp.dma_start(qT_d[bass.ds(2 * i + s, 1), :, :].rearrange("u p (k n) -> p (u k) n", k=2), QF[s])\
                            .then_inc(q_stored.sems[s], 16)

                if n == 1:
                    load_sorted(1)
                pairs(sp, store_a1)
                enter(sp, f"B1.{n}")
                wait(sp, context(f"A1.{n}", "cleared"))
                if n + 1 < LAYERS:
                    load_l1(n + 1)
                else:
                    load("C1a", (w1_gnn, byk(a["L1_gnn_weight"])))

                def load_b1(i, slots, phase=f"B1.{n}"):
                    for s in slots:
                        if not first(i):
                            wait(sp, pe_done.done(phase, "att", i - 1, s))
                        sp.dma_start(QF[s], qT_d[bass.ds(2 * i + s, 1), :, :]
                                     .rearrange("u p (k n) -> p (u k) n", k=2)).then_inc(q_loaded.sems[s], 16)

                pairs(sp, load_b1)

            enter(sp, "C1a")

            def load_c1a(i, slots):
                for s in slots:
                    if not first(i):
                        wait(sp, pe_done.done("C1a", "hT", i - 1, s))
                    sp.dma_start(ZT[s], tiles(xn1_d)[:, bass.ds(4 * i + 2 * s, 2), :])\
                        .then_inc(z_loaded.sems[s], 16)
                    if not first(i):
                        wait(sp, dve_done.done("C1a", "x3", i - 1, s))
                    sp.dma_start(XC[s], tiles(x2_d)[:, bass.ds(4 * i + 2 * s, 2), :])\
                        .then_inc(x_loaded.sems[s], 16)

            pairs(sp, load_c1a)

            enter(sp, "C1b")
            load("C1b", (bexp1, a["L1_ffn_expert_b3"]), (w1_rh, byk(a["L1_ffn_router_w1"])),
                 (w1_router[:, 0, :], a["L1_ffn_router_w2"]),
                 *[(w1_exp[m][e], byk(a[f"L1_ffn_expert_w{m + 1}"][e])) for e in range(NEXP1) for m in range(3)])

            def store_c1b(i, slots):
                for s in slots:
                    wait(sp, dve_done.done("C1b", f"y{NEXP1 - 1}", i, s))
                    sp.dma_start(tiles(out)[:, bass.ds(4 * i + 2 * s, 2), :], KT[s])\
                        .then_inc(k_stored.sems[s], 16)

            pairs(sp, store_c1b)
            for s in range(2):
                wait(sp, k_stored.done("C1b", NP - 1 - s, s))

        @block.gpsimd
        def _(pool):
            def made(ins):
                ins.then_inc(consts_made, 1)

            def select_where(m, compare, fill, base_, pattern, mult):
                made(nc.gpsimd.affine_select(out=m, in_=m, compare_op=compare, fill=fill, base=base_,
                                             pattern=pattern, channel_multiplier=mult))

            made(nc.gpsimd.iota(iota_b[:], pattern=[[1, NT]], base=0, channel_multiplier=0,
                                allow_small_or_imprecise_dtypes=True))
            made(nc.gpsimd.iota(iota_g, pattern=[[1, NG]], base=0, channel_multiplier=0,
                                allow_small_or_imprecise_dtypes=True))
            made(nc.gpsimd.memset(ones[:], 1.0))
            made(nc.gpsimd.memset(lower[:], 1.0))
            made(nc.gpsimd.memset(ident[:], 0.0))
            pool.wait_ge(consts_made, 5)
            select_where(lower[:], ALU.is_ge, 0.0, -1, [[1, 128]], -1)
            select_where(ident[:], ALU.not_equal, 1.0, 0, [[-1, 128]], 1)
            made(nc.gpsimd.memset(srec[:], 0.0))
            pool.wait_ge(consts_made, 8)
            made(nc.gpsimd.memset(srec[:, :, 1:2], -1.0))
            pool.wait_ge(consts_made, 9)
            for e in range(2):
                pool.dma_start(sorted_d[e].rearrange("(p t) c -> p t c", p=128), srec[:]).then_inc(blanked, 16)
            made(nc.gpsimd.iota(iota_t[:], pattern=[[1, T]], base=0, channel_multiplier=0,
                                allow_small_or_imprecise_dtypes=True))
            made(nc.gpsimd.iota(iota32[:], pattern=[[1, NEXP]], base=0, channel_multiplier=0,
                                allow_small_or_imprecise_dtypes=True))
            made(nc.gpsimd.memset(VT[:], 1.0))
            made(nc.gpsimd.memset(blocks[:], 0.0))
            made(nc.gpsimd.memset(CTX[:], 0.0))
            pool.wait_ge(consts_made, 14)
            for h in range(4):
                made(nc.gpsimd.memset(blocks[32 * h:32 * h + 32, 32 * h:32 * h + 32], 1.0))
            pool.wait_ge(consts_made, 18)
            nc.gpsimd.memset(rows[:, :, D:D + 1], 1.0).then_inc(row_free, RING)

            copies = [0]

            def scatter(e):
                pool.wait_ge(blanked, 32)
                if e == 0:
                    pool.wait_ge(sort_step, SORT_STEPS)
                    p_all, r_all = pos[0], rec[0]
                else:
                    pool.wait_ge(unspilled, 32)
                    p_all, r_all = pos1_again, rec1_again
                c0 = copies[0]

                def both_halves(i):
                    for h in range(2):
                        at = i * (2 * RING) + h * RING
                        if e or not first(i):
                            pool.wait_ge(scattered[h], i * (16 * RING) + e * 16 * EC // 2)
                        nc.gpsimd.tensor_copy(ring_idx[0:T, h, :], p_all[:, bass.ds(at, RING)])\
                            .then_inc(ring_copied, 1)
                        nc.gpsimd.tensor_copy(ring_rec[:, h, :], r_all[:, bass.ds(3 * at, 3 * RING)])\
                            .then_inc(ring_copied, 1)
                        settled(i * 4 + (c0 + 2 * h + 2))
                        for q in range(RING):
                            nc.gpsimd.indirect_dma_start(
                                out=sorted_d[e], out_offset=bass.IndirectOffsetOnAxis(
                                    ap=ring_idx[0:T, h, q:q + 1], axis=0),
                                in_=ring_rec[:, h, 3 * q:3 * q + 3], in_offset=None).then_inc(scattered[h], 16)

                both_halves(0)
                with pool.Fori(1, EC // (2 * RING)) as i:
                    both_halves(i)
                copies[0] += 4 * (EC // (2 * RING))

            def settled(count):
                pool.wait_ge(ring_copied, count)
                hold(pool)

            def gather(e, table):
                pool.wait_ge(srec_loaded, 16 * (e + 1))
                c0 = copies[0]
                with pool.Fori(0, NS // (2 * RING)) as i:
                    for h in range(2):
                        at = i * (2 * RING) + h * RING
                        nc.gpsimd.tensor_copy(ring_idx[:, h, :],
                                              srec[:, bass.ds(at, RING), 0:1].bitcast(U32)
                                              .rearrange("p t u -> p (t u)")).then_inc(ring_copied, 1)
                        settled(i * 2 + (c0 + h + 1))
                        for q in range(RING):
                            pool.wait_ge(row_free, at + (e * NS + q + 1))
                            hold(pool)
                            nc.gpsimd.indirect_dma_start(
                                out=rows[:, q, 0:D], out_offset=None, in_=table,
                                in_offset=bass.IndirectOffsetOnAxis(ap=ring_idx[:, h, q:q + 1], axis=0))\
                                .then_inc(gathered[q], 16)
                copies[0] += 2 * (NS // (2 * RING))

            scatter(0)
            wait_all = z_stored.all("B0")
            for mark in wait_all:
                wait(pool, mark)
            gather(0, xn0_d)
            wait(pool, pe_done.all("C0a"))
            wait(pool, dve_done.all("C0a"))
            made(nc.gpsimd.memset(select, MASKED))
            pool.wait_ge(consts_made, 19)
            select_where(select, ALU.is_ge, 0.0, 0, [[1, NEXP * HEXP]], -HEXP)
            pool.wait_ge(consts_made, 20)
            select_where(select, ALU.is_ge, 0.0, HEXP - 1, [[-1, NEXP * HEXP]], HEXP)
            scatter(1)
            for mark in z_stored.all("A1.0"):
                wait(pool, mark)
            gather(1, xn1_d)

        @block.scalar
        def _(act):
            def move(dst, source, func=ACT.Copy, **k):
                return nc.scalar.activation(dst, source, func, **k)

            act.wait_ge(consts_turned, 1)
            move(cols[:], PC[0][:, 0:n_cols]).then_inc(consts_turned, 1)
            move(w0_router[:], PC[0][:, 128:128 + 2 * NEXP].rearrange("p (k e) -> p k e", k=2)).then_inc(consts_turned, 1)
            act.wait_ge(consts_turned, 3)
            act.wait_ge(consts_made, 18)

            def body_a0(i, slots):
                for s in slots:
                    wait(act, pe_done.done("A0", "zT", i, s))
                    if not first(i):
                        wait(act, f_stored.done("A0", i - 1, s))
                    move(FT[s], pfeat(PA[s])).then_inc(*act_done.add("A0", "zT", slots, s))
                for s in slots:
                    wait(act, pe_done.done("A0", "v", i, s))
                    for k in range(2):
                        ins = move(VT[:, s, :, k, 0:128], ptok(PC[s])[:, :, 128 * k:128 * k + 128], scale=1.0 / N)
                    ins.then_inc(*act_done.add("A0", "v", slots, s))
                for name, x in (("k", KT), ("q", QT)):
                    for s in slots:
                        wait(act, dve_done.done("A0", name + "min", i, s))
                        move(x[s], x[s], ACT.Exp).then_inc(*act_done.add("A0", name + "exp", slots, s))

            pairs(act, body_a0)

            def make_context(phase):
                wait(act, context(phase, "turned"))
                if phase == "A0":
                    move(KSB, PC[0][0:T, 0:D])
                move(CNT, PA[0][:, 0:256].rearrange("p (k n) -> p k n", k=2)).then_inc(context_step, 1)
                wait(act, context(phase, "times_w"))
                move(MM[:], PB[0][:, :].rearrange("p (k n) -> p k n", k=2)).then_inc(context_step, 1)

            make_context("A0")
            enter(act, "B0")

            def body_b0(i, slots):
                for s in slots:
                    wait(act, pe_done.done("B0", "qT", i, s))
                    move(QF[s], pfeat(PA[s])).then_inc(*act_done.add("B0", "qT", slots, s))
                for s in slots:
                    wait(act, pe_done.done("B0", "mT", i, s))
                    for k in range(2):
                        ins = move(QF[s][:, k, :], pfeat(PA[s])[:, k, :], ACT.Identity,
                                   bias=col("b1", k), scale=col("g1", k))
                    ins.then_inc(*act_done.add("B0", "mT", slots, s))
                for h, P in enumerate((PB, PC)):
                    for s in slots:
                        wait(act, pe_done.done("B0", f"h{h}", i, s))
                        move(HT[:, s, 2 * h:2 * h + 2, :], pfeat(P[s]), ACT.Relu)\
                            .then_inc(*act_done.add("B0", f"h{h}", slots, s))

            pairs(act, body_b0)
            enter(act, "C0a")

            def body_c0a(i, slots):
                for s in slots:
                    wait(act, pe_done.done("C0a", "hT", i, s))
                    move(FT[s], pfeat(PA[s])).then_inc(*act_done.add("C0a", "hT", slots, s))
                for h, P in enumerate((PB, PC)):
                    for s in slots:
                        wait(act, pe_done.done("C0a", f"h{h}", i, s))
                        for b in range(2):
                            ins = move(HT[:, s, 2 * h + b, :], pfeat(P[s])[:, b, :], ACT.Relu,
                                       bias=col("gnn_b1", 2 * h + b))
                        ins.then_inc(*act_done.add("C0a", f"h{h}", slots, s))

            pairs(act, body_c0a)
            enter(act, "C0b")

            def body_c0b(i, slots):
                for s in slots:
                    wait(act, pe_done.done("C0b", "zT", i, s))
                    move(FT[s], pfeat(PA[s])).then_inc(*act_done.add("C0b", "zT", slots, s))
                for p in range(8):
                    for s in slots:
                        wait(act, pe_done.done("C0b", f"h{p}", i, s))
                        for b in range(2):
                            ins = move(HT[:, s, (2 * p + b) % 8, :], pfeat((PB, PC)[p % 2][s])[:, b, :], ACT.Relu,
                                       bias=col("exp_b1", 2 * p + b))
                        ins.then_inc(*act_done.add("C0b", f"h{p}", slots, s))
                for s in slots:
                    wait(act, dve_done.done("C0b", "xn", i, s))
                    move(XM[:, bass.ds(4 * i + 2 * s, 2), :], ZT[s]).then_inc(*act_done.add("C0b", "xm", slots, s))

            pairs(act, body_c0b)

            for n in range(LAYERS):
                def body_a1(i, slots, phase=f"A1.{n}", n=n):
                    for s in slots:
                        wait(act, pe_done.done(phase, "zT", i, s))
                        for k in range(2):
                            ins = move(FT[s][:, k, :], pfeat(PA[s])[:, k, :], ACT.Identity,
                                       bias=col("ln1_b", 2 * n + k), scale=col("ln1_g", 2 * n + k))
                        ins.then_inc(*act_done.add(phase, "zT", slots, s))
                    for s in slots:
                        wait(act, pe_done.done(phase, "v", i, s))
                        for k in range(2):
                            ins = move(VT[:, s, :, k, 0:128], ptok(PC[s])[:, :, 128 * k:128 * k + 128])
                        ins.then_inc(*act_done.add(phase, "v", slots, s))
                    wait(act, dve_done.done(phase, "drop", i))
                    move(AL[:], AL[:], ACT.Exp, scale=SCALE).then_inc(*act_done.add(phase, "drop", slots))
                    for s in slots:
                        for k in range(2):
                            ins = move(PF[s][:, k, :], pfeat(PB[s])[:, k, :], ACT.Exp,
                                       bias=NEG[:, k:k + 1], scale=SCALE)
                        ins.then_inc(*act_done.add(phase, "kexp", slots, s))
                    for s in slots:
                        wait(act, dve_done.done(phase, "qsub", i, s))
                        move(QT[s], QT[s], ACT.Exp, scale=SCALE).then_inc(*act_done.add(phase, "qexp", slots, s))
                    for s in slots:
                        wait(act, pe_done.done(phase, "qT", i, s))
                        if not first(i):
                            wait(act, q_stored.done(phase, i - 1, s))
                        move(QF[s], pfeat(PA[s])).then_inc(*act_done.add(phase, "qT", slots, s))

                enter(act, f"A1.{n}")
                pairs(act, body_a1)
                make_context(f"A1.{n}")
                enter(act, f"B1.{n}")

                def body_b1(i, slots, phase=f"B1.{n}", n=n):
                    for s in slots:
                        wait(act, pe_done.done(phase, "zT", i, s))
                        for k in range(2):
                            ins = move(FT[s][:, k, :], pfeat(PB[s])[:, k, :], ACT.Identity,
                                       bias=col("ln2_b", 2 * n + k), scale=col("ln2_g", 2 * n + k))
                        ins.then_inc(*act_done.add(phase, "zT", slots, s))
                    for p in range(4):
                        for s in slots:
                            wait(act, pe_done.done(phase, f"h{p}", i, s))
                            for b in range(2):
                                ins = move(HT[:, s, 2 * p + b, :], pfeat((PB, PC)[p % 2][s])[:, b, :], ACT.Gelu,
                                           bias=col("up_b", 8 * n + 2 * p + b))
                            ins.then_inc(*act_done.add(phase, f"h{p}", slots, s))

                pairs(act, body_b1)

            enter(act, "C1a")

            def body_c1a(i, slots):
                for s in slots:
                    wait(act, pe_done.done("C1a", "hT", i, s))
                    move(FT[s], pfeat(PA[s])).then_inc(*act_done.add("C1a", "hT", slots, s))

            pairs(act, body_c1a)
            enter(act, "C1b")

            def body_c1b(i, slots):
                for s in slots:
                    wait(act, pe_done.done("C1b", "zT", i, s))
                    move(FT[s], pfeat(PA[s])).then_inc(*act_done.add("C1b", "zT", slots, s))
                for s in slots:
                    wait(act, pe_done.done("C1b", "rh", i, s))
                    move(QF[s][:, 0, :], PB[s][:, 0:CH], ACT.Relu, bias=col("rh_b", 0))\
                        .then_inc(*act_done.add("C1b", "rh", slots, s))
                for s in slots:
                    wait(act, dve_done.done("C1b", "lsub", i, s))
                    move(LG[:, s, :, 0:NEXP1], LG[:, s, :, 0:NEXP1], ACT.Exp)\
                        .then_inc(*act_done.add("C1b", "pexp", slots, s))
                for s in slots:
                    wait(act, dve_done.done("C1b", "gdif", i, s))
                    move(GD[:, s, :], GD[:, s, :], ACT.Exp).then_inc(*act_done.add("C1b", "gexp", slots, s))
                for s in slots:
                    wait(act, pe_done.done("C1b", "gT", i, s))
                    move(GT[0:8, s, :], PB[s][0:8, 0:CH]).then_inc(*act_done.add("C1b", "gT", slots, s))
                for e in range(NEXP1):
                    for m, P, name in ((0, PB, "a"), (1, PC, "b")):
                        for s in slots:
                            wait(act, pe_done.done("C1b", f"{name}{e}", i, s))
                            for b in range(2):
                                ins = move(HT[:, s, 4 * (e % 2) + 2 * m + b, :], pfeat(P[s])[:, b, :], ACT.Relu,
                                           bias=col(f"exp1_b{m + 1}", 2 * e + b))
                            ins.then_inc(*act_done.add("C1b", f"{name}{e}", slots, s))

            pairs(act, body_c1b)

        @block.vector
        def _(dve):
            def self_wait(phase, stage, i, s=1):
                wait(dve, dve_done.done(phase, stage, i, s))

            def rsqrt(v, y, t, half_bits, mark):
                mark(1, nc.vector.tensor_scalar(y.bitcast(I32), v.bitcast(I32), 1, None, ALU.arith_shift_right))
                mark(2, nc.vector.tensor_scalar(v, v, -0.5, None, ALU.mult))
                mark(3, nc.vector.tensor_scalar(y.bitcast(I32), y.bitcast(I32), -1, half_bits, ALU.mult, ALU.add))
                for n in range(3):
                    mark(4 + 3 * n, nc.vector.tensor_tensor(t, y, y, ALU.mult))
                    mark(5 + 3 * n, nc.vector.tensor_tensor(t, t, v, ALU.mult))
                    mark(6 + 3 * n, nc.vector.scalar_tensor_tensor(y, t, 1.5, y, ALU.add, ALU.mult))

            def norm(phase, i, slots, source, pre="", ready=None):
                n = len(slots)
                for s in slots:
                    if ready:
                        ready(s)
                    x = source(s)
                    for t in range(2):
                        ins = nc.vector.bn_stats(STAT[:, s, t, :], x[:, t, :])
                    ins.then_inc(*dve_done.add(phase, pre + "stats", slots, s))
                for s in slots:
                    self_wait(phase, pre + "stats", i, s)
                    for t in range(2):
                        if t == 0:
                            hold(dve)
                        ins = nc.vector.bn_aggr(MV[:, s, t, :], STAT[:, s, t, :])
                    ins.then_inc(*dve_done.add(phase, pre + "mean", slots, s))
                self_wait(phase, pre + "mean", i)
                v, y, t = RV[:, 0:n, :], RY[:, 0:n, :], RT[:, 0:n, :]

                def mark(k, ins):
                    ins.then_inc(*dve_done.add(phase, pre + RSQRT[k], slots))
                    self_wait(phase, pre + RSQRT[k], i)

                mark(0, nc.vector.tensor_scalar(v, MV[:, 0:n, :, 1], EPS, None, ALU.add))
                rsqrt(v, y, t, GUESS, mark)

            def normed(s, dst, x, t):
                return nc.vector.tensor_scalar(dst[:, t, :], x[:, t, :], MV[:, s, t, 0:1], RY[:, s, t:t + 1],
                                               ALU.subtract, ALU.mult)

            def state(i, s):
                return XM[:, bass.ds(4 * i + 2 * s, 2), :]

            dve.wait_ge(edges_loaded, 48)

            def sort(e):
                count = [e * SORT_STEPS]

                def step(ins):
                    ins.then_inc(sort_step, 1)
                    count[0] += 1
                    dve.wait_ge(sort_step, count[0])

                key, other = ((src_i, dst_i), (dst_i, src_i))[e]
                fields = rec[e].rearrange("p (c f) -> p c f", f=3)
                def field(n):
                    return fields[:, :, n:n + 1].rearrange("p c u -> p (c u)")
                if e == 0:
                    dve.wait_ge(consts_made, 7)
                step(nc.vector.tensor_copy(keyf, key))
                step(nc.vector.tensor_scalar(blk, keyf, float((T - 1) / 2), 1.0 / T, ALU.subtract, ALU.mult))
                step(nc.vector.tensor_scalar(blk, blk, ROUND, ROUND, ALU.add, ALU.subtract))
                step(nc.vector.scalar_tensor_tensor(field(1), blk, float(-T), keyf, ALU.mult, ALU.add))
                step(nc.vector.tensor_copy(field(0).bitcast(I32), other))
                if e == 0:
                    step(nc.vector.tensor_copy(field(2), ew))
                else:
                    step(nc.vector.memset(field(2), 1.0))
                step(nc.vector.memset(rank, 0.0))
                step(nc.vector.memset(start, 0.0))
                step(nc.vector.memset(tmp, 0.0))
                c0 = count[0]
                with dve.Fori(0, NT) as b:
                    dve.wait_ge(sort_step, b * 4 + c0)
                    nc.vector.tensor_scalar(is_b, blk, iota_b[:, bass.ds(b, 1)], None, ALU.is_equal)\
                        .then_inc(sort_step, 1)
                    dve.wait_ge(sort_step, b * 4 + (c0 + 1))
                    nc.vector.tensor_tensor_scan(scan, is_b, tmp, 0.0, ALU.add, ALU.add).then_inc(sort_step, 1)
                    dve.wait_ge(sort_step, b * 4 + (c0 + 2))
                    nc.vector.tensor_copy(tot[:, bass.ds(b, 1)], scan[:, EC - 1:EC]).then_inc(sort_step, 1)
                    dve.wait_ge(sort_step, b * 4 + (c0 + 2))
                    hold(dve)
                    nc.vector.copy_predicated(rank, is_b.bitcast(I32), scan).then_inc(sort_step, 1)
                count[0] += 4 * NT
                dve.wait_ge(sort_step, count[0])
                TOT, BEFORE, TOTT, GENDT, GB_ = (PA[1][0:T, 0:NT], PB[1][0:T, 0:NT], PC[1][0:NT, 0:1],
                                                 PA[1][0:NT, 0:1], PB[1][0:1, 0:NG])
                dve.wait_ge(sort_sums, 3 * e + 1)
                to_groups = (1.0 / GR, (GR - 1) / (2.0 * GR))
                step(nc.vector.tensor_scalar(gr, TOT, *to_groups, ALU.mult, ALU.add))
                step(nc.vector.tensor_scalar(gr, gr, ROUND, ROUND, ALU.add, ALU.subtract))
                step(nc.vector.tensor_tensor_scan(gend, gr, tmp[:, 0:NT], 0.0, ALU.add, ALU.add))
                step(nc.vector.tensor_tensor(base, gend, gr, ALU.subtract))
                step(nc.vector.scalar_tensor_tensor(base, base, float(GR), BEFORE, ALU.mult, ALU.add))
                step(nc.vector.tensor_scalar(grT[:], TOTT, *to_groups, ALU.mult, ALU.add))
                step(nc.vector.tensor_scalar(grT[:], grT[:], ROUND, ROUND, ALU.add, ALU.subtract))
                c0 = count[0]
                with dve.Fori(0, NT) as b:
                    dve.wait_ge(sort_step, b * 2 + c0)
                    nc.vector.tensor_scalar(is_b, blk, iota_b[:, bass.ds(b, 1)], base[:, bass.ds(b, 1)],
                                            ALU.is_equal, ALU.mult).then_inc(sort_step, 1)
                    dve.wait_ge(sort_step, b * 2 + (c0 + 1))
                    nc.vector.tensor_tensor(start, start, is_b, ALU.add).then_inc(sort_step, 1)
                count[0] += 2 * NT
                dve.wait_ge(sort_step, count[0])
                step(nc.vector.scalar_tensor_tensor(start, start, -1.0, rank, ALU.add, ALU.add))
                step(nc.vector.tensor_scalar(lane, start, 63.5, 1.0 / 128, ALU.subtract, ALU.mult))
                step(nc.vector.tensor_scalar(lane, lane, ROUND, ROUND, ALU.add, ALU.subtract))
                step(nc.vector.scalar_tensor_tensor(start, lane, -128.0, start, ALU.mult, ALU.add))
                step(nc.vector.scalar_tensor_tensor(start, start, float(NS), lane, ALU.mult, ALU.add))
                step(nc.vector.tensor_copy(pos[e], start))
                dve.wait_ge(sort_sums, 3 * e + 2)
                step(nc.vector.tensor_tensor(gendT[:], GENDT, grT[:], ALU.add))
                step(nc.vector.tensor_scalar(gcmp, iota_g, gendT[:], None, ALU.is_ge))
                dve.wait_ge(sort_sums, 3 * e + 3)
                step(nc.vector.tensor_scalar(gblk[:, e, :], GB_, float(NT - 1), None, ALU.min))
                assert count[0] == (e + 1) * SORT_STEPS, count

            sort(0)
            dve.wait_ge(consts_loaded, 16 * (len(vectors) + 3))
            dve.wait_ge(consts_made, 18)

            def body_a0(i, slots):
                norm("A0", i, slots, lambda s: XC[s], ready=lambda s: wait(dve, x_loaded.done("A0", i, s)))
                for s in slots:
                    if not first(i):
                        wait(dve, pe_done.done("A0", "zT", i - 1, s))
                        wait(dve, z_stored.done("A0", i - 1, s))
                    normed(s, ZT[s], XC[s], 0)
                    normed(s, ZT[s], XC[s], 1).then_inc(*dve_done.add("A0", "z", slots, s))
                for s in slots:
                    wait(dve, pe_done.done("A0", "k", i, s))
                    nc.vector.tensor_scalar(KT[s], ptok(PB[s]), 0.0, None, ALU.min)\
                        .then_inc(*dve_done.add("A0", "kmin", slots, s))
                for s in slots:
                    wait(dve, pe_done.done("A0", "q", i, s))
                    if not first(i):
                        wait(dve, q_stored.done("A0", i - 1, s))
                    nc.vector.tensor_scalar(QT[s], ptok(PA[s]), 0.0, None, ALU.min)\
                        .then_inc(*dve_done.add("A0", "qmin", slots, s))
                for name, x, P in (("k", KT, PB), ("q", QT, PA)):
                    for s in slots:
                        wait(dve, act_done.done("A0", name + "exp", i, s))
                        nc.vector.scalar_tensor_tensor(x[s], ptok(P[s]), 0.0, x[s], ALU.max, ALU.add)\
                            .then_inc(*dve_done.add("A0", name, slots, s))
                for s in slots:
                    wait(dve, pe_done.done("A0", "ctx", i, s))
                    if s == 1:
                        self_wait("A0", "ctx", i, 0)
                    elif not first(i):
                        self_wait("A0", "ctx", i - 1, 1)
                    nc.vector.tensor_tensor(CTX[:], CTX[:], PB[s][:, :].rearrange("p (k n) -> p k n", k=2)[:, :, 0:129],
                                            ALU.add).then_inc(*dve_done.add("A0", "ctx", slots, s))

            pairs(dve, body_a0)
            self_wait("A0", "ctx", NP - 1)

            def make_context(phase):
                if phase == "A0":
                    for k in range(2):
                        ins = nc.vector.tensor_scalar(KD[:, k, :], ident[:], CTX[:, k, 128:129], None, ALU.mult)
                    ins.then_inc(context_step, 1)
                    for k in range(2):
                        ins = nc.vector.scalar_tensor_tensor(CN[:, k, :], CTX[:, k, 0:128], float(N), blocks[:],
                                                             ALU.mult, ALU.mult)
                else:
                    nc.vector.reciprocal(KR[:], CTX[:, :, 128:129]).then_inc(context_step, 1)
                    wait(dve, context(phase, "scaled"))
                    for k in range(2):
                        ins = nc.vector.scalar_tensor_tensor(CN[:, k, :], CTX[:, k, 0:128], KR[:, k, :], blocks[:],
                                                             ALU.mult, ALU.mult)
                ins.then_inc(context_step, 1)
                wait(dve, context(phase, "ready"))
                nc.vector.memset(RUN[:], LOWEST)
                nc.vector.memset(CTX[:], 0.0).then_inc(context_step, 1)
                wait(dve, context(phase, "cleared"))

            make_context("A0")
            enter(dve, "B0")
            dve.wait_ge(weights_loaded["B0"], weight_loads["B0"])
            nc.vector.tensor_tensor(rowB[:], rowB[:], rowC, ALU.add).then_inc(degree_step, 1)
            dve.wait_ge(degree_step, 1)

            def body_b0(i, slots):
                for s in slots:
                    wait(dve, q_loaded.done("B0", i, s))
                    if not first(i):
                        wait(dve, pe_done.done("B0", "mT", i - 1, s))
                        self_wait("B0", "r", i - 1, s)
                    nc.vector.tensor_tensor(TM[s], QT[s], both(KSB), ALU.mult)\
                        .then_inc(*dve_done.add("B0", "prod", slots, s))
                for s in slots:
                    self_wait("B0", "prod", i, s)
                    nc.vector.tensor_reduce(DN[:, s, :], heads(TM[s]), AX.X, ALU.add)\
                        .then_inc(*dve_done.add("B0", "den", slots, s))
                for s in slots:
                    self_wait("B0", "den", i, s)
                    nc.vector.tensor_scalar(DN[:, s, :], DN[:, s, :], ATT_EPS, None, ALU.add)\
                        .then_inc(*dve_done.add("B0", "deneps", slots, s))
                for s in slots:
                    self_wait("B0", "deneps", i, s)
                    nc.vector.reciprocal(DN[:, s, :], DN[:, s, :]).then_inc(*dve_done.add("B0", "denrec", slots, s))
                for s in slots:
                    self_wait("B0", "denrec", i, s)
                    nc.vector.tensor_tensor(heads(QT[s]), heads(QT[s]), per_head(s), ALU.mult)\
                        .then_inc(*dve_done.add("B0", "q", slots, s))
                norm("B0", i, slots, lambda s: ptok(PB[s]), ready=lambda s: wait(dve, pe_done.done("B0", "msg", i, s)))
                for s in slots:
                    normed(s, TM[s], ptok(PB[s]), 0)
                    normed(s, TM[s], ptok(PB[s]), 1).then_inc(*dve_done.add("B0", "m", slots, s))
                norm("B0", i, slots, lambda s: ptok(PA[s]), "o",
                     ready=lambda s: wait(dve, pe_done.done("B0", "out", i, s)))
                for s in slots:
                    normed(s, TM[s], ptok(PA[s]), 0)
                    normed(s, TM[s], ptok(PA[s]), 1).then_inc(*dve_done.add("B0", "oz", slots, s))
                for s in slots:
                    self_wait("B0", "oz", i, s)
                    nc.vector.tensor_tensor(TM[s], TM[s], both(rowA[:]), ALU.mult)\
                        .then_inc(*dve_done.add("B0", "og", slots, s))
                for s in slots:
                    self_wait("B0", "og", i, s)
                    wait(dve, z_loaded.done("B0", i, s))
                    nc.vector.tensor_tensor(TM[s], TM[s], ZT[s], ALU.add)\
                        .then_inc(*dve_done.add("B0", "ox", slots, s))
                for s in slots:
                    self_wait("B0", "ox", i, s)
                    wait(dve, x_loaded.done("B0", i, s))
                    nc.vector.tensor_tensor(TM[s], TM[s], XC[s], ALU.add)\
                        .then_inc(*dve_done.add("B0", "or", slots, s))
                for s in slots:
                    self_wait("B0", "or", i, s)
                    if not first(i):
                        wait(dve, k_stored.done("B0", i - 1, s))
                    nc.vector.tensor_tensor(KT[s], TM[s], both(rowB[:]), ALU.add)\
                        .then_inc(*dve_done.add("B0", "r", slots, s))

            pairs(dve, body_b0)
            sort(1)
            dve.wait_ge(sort_step, 2 * SORT_STEPS)
            nc.vector.memset(zero[:], 0.0)
            nc.vector.memset(agg_all[0:T, :], 0.0).then_inc(agg_zeroed, 1)
            dve.wait_ge(agg_zeroed, 1)

            def one_hots(e, turn, u0, u1):
                for u in range(u0, u1):
                    dve.wait_ge(row_free, turn * RING + (e * NS + u + 1))
                    at = turn * RING + u
                    nc.vector.tensor_scalar(onehot[:, u, :], iota_t[:],
                                            srec[:, bass.ds(at, 1), 1:2].rearrange("p t u -> p (t u)"),
                                            srec[:, bass.ds(at, 1), 2:3].rearrange("p t u -> p (t u)"),
                                            ALU.is_equal, ALU.mult).then_inc(onehot_made, 1)

            def add_groups(e, turn, g0, g1):
                for g in range(g0, g1):
                    b = dve.value_load(gblk[0:1, e, bass.ds(turn * GROUPS + g, 1)], min_val=0, max_val=NT - 1)
                    dve.wait_ge(row_free, turn * RING + (e * NS + RING + 2 * g + 2))
                    dve.wait_ge(group_added, turn * GROUPS + (e * NG + 2 + g))
                    sums = AGG[:, bass.ds(b, 1), :]
                    nc.vector.tensor_tensor(sums, sums, PSUMS[g % 2][0:T, 0:D + 1].rearrange("p (u n) -> p u n", u=1),
                                            ALU.add).then_inc(group_added, 1)

            def one_hots_beside(phase, i, k):
                turn, n = turns(phase, i)
                if k < n:
                    one_hots(1, turn + k, 0, RING)

            def add_groups_beside(phase, i, k, g0, g1):
                turn, n = turns(phase, i)
                if k < n:
                    add_groups(1, turn + k, g0, g1)

            def sum_edges(e):
                dve.wait_ge(srec_loaded, 16 * (e + 1))
                one_hots(e, 0, 0, RING)
                with dve.Fori(0, NS // RING - 1) as i:
                    for g in range(GROUPS):
                        add_groups(e, i, g, g + 1)
                        one_hots(e, i + 1, 2 * g, 2 * g + 2)
                add_groups(e, NS // RING - 1, 0, GROUPS)
                dve.wait_ge(group_added, (e + 1) * NG + 2)

            nc.vector.memset(GA[:], 0.0).then_inc(group_added, 2)
            sum_edges(0)
            enter(dve, "C0a")
            dve.wait_ge(spilled, 32)

            def body_c0a(i, slots):
                for s in slots:
                    wait(dve, z_loaded.done("C0a", i, s))
                    nc.vector.tensor_tensor(ZT[s], ZT[s], AGG[:, bass.ds(4 * i + 2 * s, 2), 0:D], ALU.add)\
                        .then_inc(*dve_done.add("C0a", "h", slots, s))
                for s in slots:
                    wait(dve, pe_done.done("C0a", "out", i, s))
                    wait(dve, x_loaded.done("C0a", i, s))
                    nc.vector.tensor_tensor(state(i, s), XC[s], ptok(PA[s]), ALU.add)\
                        .then_inc(*dve_done.add("C0a", "x1", slots, s))

            pairs(dve, body_c0a)
            enter(dve, "C0b")

            def body_c0b(i, slots):
                norm("C0b", i, slots, lambda s: state(i, s))
                for s in slots:
                    if not first(i):
                        wait(dve, z_stored.done("C0b", i - 1, s))
                        wait(dve, act_done.done("C0b", "xm", i - 1, s))
                    normed(s, ZT[s], state(i, s), 0)
                    normed(s, ZT[s], state(i, s), 1).then_inc(*dve_done.add("C0b", "z", slots, s))
                for s in slots:
                    wait(dve, pe_done.done("C0b", "logit", i, s))
                    nc.vector.tensor_tensor(LG[:, s, :, :], PC[s][0:T, 0:2 * NEXP].rearrange("p (t e) -> p t e", t=2),
                                            rowR[:].rearrange("p (u e) -> p u e", u=1).to_broadcast([T, 2, NEXP]),
                                            ALU.add).then_inc(*dve_done.add("C0b", "logit", slots, s))
                for s in slots:
                    self_wait("C0b", "logit", i, s)
                    hold(dve)
                    for t in range(2):
                        ins = nc.vector.max(MX[:, s, t, :], LG[:, s, t, :])
                    ins.then_inc(*dve_done.add("C0b", "max", slots, s))
                for s in slots:
                    self_wait("C0b", "max", i, s)
                    hold(dve)
                    for t in range(2):
                        ins = nc.vector.max_index(IX[:, s, t, :], MX[:, s, t, :], LG[:, s, t, :])
                    ins.then_inc(*dve_done.add("C0b", "arg", slots, s))
                for s in slots:
                    self_wait("C0b", "arg", i, s)
                    nc.vector.tensor_copy(IXF[:, s, :, :], IX[:, s, :, :]).then_inc(*dve_done.add("C0b", "argf", slots, s))
                for s in slots:
                    self_wait("C0b", "argf", i, s)
                    for t in range(2):
                        ins = nc.vector.tensor_scalar(OH[:, s, t, :], iota32[:], IXF[:, s, t, 0:1], None, ALU.is_equal)
                    ins.then_inc(*dve_done.add("C0b", "one", slots, s))
                for s in slots:
                    wait(dve, pe_done.done("C0b", "oneT", i, s))
                    nc.vector.tensor_copy(OHT[:, s, :], PB[s][0:NEXP, 0:CH]).then_inc(*dve_done.add("C0b", "oneT", slots, s))
                for s in slots:
                    nc.vector.tensor_scalar(OHM[:, s, :], PB[s][0:NEXP, 0:CH], -1.0, None, ALU.add)\
                        .then_inc(*dve_done.add("C0b", "mask", slots, s))
                for s in slots:
                    wait(dve, pe_done.done("C0b", "out", i, s))
                    if not first(i):
                        wait(dve, x_stored.done("C0b", i - 1, s))
                    nc.vector.scalar_tensor_tensor(XC[s], ptok(PA[s]), 0.0, state(i, s), ALU.max, ALU.add)\
                        .then_inc(*dve_done.add("C0b", "x2", slots, s))
                norm("C0b", i, slots, lambda s: XC[s], "n", ready=lambda s: (self_wait("C0b", "x2", i, s),
                                                                            hold(dve)))
                for s in slots:
                    normed(s, ZT[s], XC[s], 0)
                    normed(s, ZT[s], XC[s], 1).then_inc(*dve_done.add("C0b", "xn", slots, s))

            pairs(dve, body_c0b)
            enter(dve, "A1.0")

            for n in range(LAYERS):
                def body_a1(i, slots, phase=f"A1.{n}"):
                    norm(phase, i, slots, lambda s: state(i, s))
                    for s in slots:
                        if not first(i):
                            wait(dve, pe_done.done(phase, "zT", i - 1, s))
                        normed(s, ZT[s], state(i, s), 0)
                        normed(s, ZT[s], state(i, s), 1).then_inc(*dve_done.add(phase, "z", slots, s))
                    one_hots_beside(phase, i, 0)
                    for s in slots:
                        wait(dve, pe_done.done(phase, "k", i, s))
                        nc.vector.tensor_reduce(KM[:, s, :], pfeat(PB[s]), AX.X, ALU.max)\
                            .then_inc(*dve_done.add(phase, "kmax", slots, s))
                    self_wait(phase, "kmax", i)
                    nc.vector.tensor_tensor(NM[:], KM[:, 0, :], KM[:, slots[-1], :], ALU.max)\
                        .then_inc(*dve_done.add(phase, "pairmax", slots))
                    self_wait(phase, "pairmax", i)
                    nc.vector.tensor_tensor(NM[:], NM[:], RUN[:], ALU.max).then_inc(*dve_done.add(phase, "runmax", slots))
                    self_wait(phase, "runmax", i)
                    if not first(i):
                        wait(dve, act_done.done(phase, "kexp", i - 1))
                        self_wait(phase, "ctx", i - 1)
                    nc.vector.tensor_scalar(NEG[:], NM[:], -SCALE, None, ALU.mult)\
                        .then_inc(*dve_done.add(phase, "negmax", slots))
                    nc.vector.tensor_tensor(AL[:], RUN[:], NM[:], ALU.subtract)\
                        .then_inc(*dve_done.add(phase, "drop", slots))
                    self_wait(phase, "drop", i)
                    nc.vector.tensor_copy(RUN[:], NM[:]).then_inc(*dve_done.add(phase, "keep", slots))
                    for s in slots:
                        wait(dve, pe_done.done(phase, "kT", i, s))
                        nc.vector.tensor_copy(KT[s], ptok(PA[s])).then_inc(*dve_done.add(phase, "kT", slots, s))
                    add_groups_beside(phase, i, 0, 0, 2)
                    for s in slots:
                        wait(dve, pe_done.done(phase, "q", i, s))
                        nc.vector.tensor_reduce(DN[:, s, :], heads(ptok(PB[s])), AX.X, ALU.max)\
                            .then_inc(*dve_done.add(phase, "qmax", slots, s))
                    for s in slots:
                        self_wait(phase, "qmax", i, s)
                        nc.vector.tensor_tensor(heads(QT[s]), heads(ptok(PB[s])), per_head(s), ALU.subtract)\
                            .then_inc(*dve_done.add(phase, "qsub", slots, s))
                    for s in slots:
                        wait(dve, act_done.done(phase, "qexp", i, s))
                        nc.vector.tensor_reduce(DN[:, s, :], heads(QT[s]), AX.X, ALU.add)\
                            .then_inc(*dve_done.add(phase, "qsum", slots, s))
                    for s in slots:
                        self_wait(phase, "qsum", i, s)
                        nc.vector.reciprocal(DN[:, s, :], DN[:, s, :]).then_inc(*dve_done.add(phase, "qrec", slots, s))
                    for s in slots:
                        self_wait(phase, "qrec", i, s)
                        nc.vector.tensor_tensor(heads(QT[s]), heads(QT[s]), per_head(s), ALU.mult)\
                            .then_inc(*dve_done.add(phase, "q", slots, s))
                    for s in slots:
                        wait(dve, pe_done.done(phase, "ctx", i, s))
                        P = PC[s][:, :].rearrange("p (k n) -> p k n", k=2)[:, :, 0:129]
                        if s == 0:
                            wait(dve, act_done.done(phase, "drop", i))
                            if not first(i):
                                self_wait(phase, "ctx", i - 1)
                            for k in range(2):
                                ins = nc.vector.scalar_tensor_tensor(CTX[:, k, :], CTX[:, k, :], AL[:, k:k + 1],
                                                                     P[:, k, :], ALU.mult, ALU.add)
                        else:
                            self_wait(phase, "ctx", i, 0)
                            ins = nc.vector.tensor_tensor(CTX[:], CTX[:], P, ALU.add)
                        ins.then_inc(*dve_done.add(phase, "ctx", slots, s))
                    add_groups_beside(phase, i, 0, 2, 4)

                if n:
                    enter(dve, f"A1.{n}")
                if n == 1:
                    dve.wait_ge(agg_zeroed, 1 + NP)
                    dve.wait_ge(srec_loaded, 32)
                pairs(dve, body_a1)
                self_wait(f"A1.{n}", "ctx", NP - 1)
                make_context(f"A1.{n}")
                enter(dve, f"B1.{n}")
                if n == 0:
                    for h in range(2):
                        dve.wait_ge(scattered[h], 16 * EC)
                dve.wait_ge(weights_loaded[f"B1.{n}"], weight_loads[f"B1.{n}"])

                def body_b1(i, slots, phase=f"B1.{n}"):
                    if phase == "B1.0":
                        n_tiles = 2 * len(slots)
                        nc.vector.tensor_copy(AGG[:, bass.ds(4 * i, n_tiles), :],
                                              zero[:].rearrange("p (t n) -> p t n", t=1)
                                              .to_broadcast([T, n_tiles, D + 1])).then_inc(agg_zeroed, 1)
                    one_hots_beside(phase, i, 0)
                    for s in slots:
                        wait(dve, pe_done.done(phase, "att", i, s))
                        nc.vector.tensor_tensor(state(i, s), state(i, s), ptok(PA[s]), ALU.add)\
                            .then_inc(*dve_done.add(phase, "att", slots, s))
                    for s in slots:
                        self_wait(phase, "att", i, s)
                        nc.vector.tensor_tensor(state(i, s), state(i, s), both(rowA[:]), ALU.add)\
                            .then_inc(*dve_done.add(phase, "bo", slots, s))
                    norm(phase, i, slots, lambda s: state(i, s),
                         ready=lambda s: (self_wait(phase, "bo", i, s), hold(dve)))
                    for s in slots:
                        if not first(i):
                            wait(dve, pe_done.done(phase, "zT", i - 1, s))
                        normed(s, ZT[s], state(i, s), 0)
                        normed(s, ZT[s], state(i, s), 1).then_inc(*dve_done.add(phase, "z", slots, s))
                    add_groups_beside(phase, i, 0, 0, 4)
                    one_hots_beside(phase, i, 1)
                    add_groups_beside(phase, i, 1, 0, 4)
                    for s in slots:
                        wait(dve, pe_done.done(phase, "out", i, s))
                        nc.vector.tensor_tensor(state(i, s), state(i, s), ptok(PA[s]), ALU.add)\
                            .then_inc(*dve_done.add(phase, "out", slots, s))
                    for s in slots:
                        self_wait(phase, "out", i, s)
                        nc.vector.tensor_tensor(state(i, s), state(i, s), both(rowB[:]), ALU.add)\
                            .then_inc(*dve_done.add(phase, "b2", slots, s))

                pairs(dve, body_b1)

            dve.wait_ge(group_added, 2 * NG + 2)
            enter(dve, "C1a")

            count = [1]

            def mark(k, ins):
                ins.then_inc(degree_step, 1)
                count[0] += 1
                dve.wait_ge(degree_step, count[0])

            degrees = AGG[:, :, D:D + 1].rearrange("p t u -> p (t u)")
            mark(0, nc.vector.tensor_scalar(DG[:], degrees, 1.0, None, ALU.max))
            rsqrt(DG[:], DY[:], DT[:], GUESS, mark)

            def body_c1a(i, slots):
                for s in slots:
                    wait(dve, z_loaded.done("C1a", i, s))
                    nc.vector.tensor_tensor(ZT[s], ZT[s], AGG[:, bass.ds(4 * i + 2 * s, 2), 0:D], ALU.add)\
                        .then_inc(*dve_done.add("C1a", "h", slots, s))
                for s in slots:
                    self_wait("C1a", "h", i, s)
                    nc.vector.tensor_tensor(ZT[s], ZT[s], DY[:, bass.ds(4 * i + 2 * s, 2)]
                                            .rearrange("p (t u) -> p t u", u=1).to_broadcast([T, 2, D]), ALU.mult)\
                        .then_inc(*dve_done.add("C1a", "hs", slots, s))
                for s in slots:
                    wait(dve, x_loaded.done("C1a", i, s))
                    nc.vector.tensor_tensor(XC[s], XC[s], state(i, s), ALU.add)\
                        .then_inc(*dve_done.add("C1a", "xa", slots, s))
                for s in slots:
                    self_wait("C1a", "xa", i, s)
                    wait(dve, pe_done.done("C1a", "out", i, s))
                    nc.vector.tensor_tensor(state(i, s), XC[s], ptok(PA[s]), ALU.add)\
                        .then_inc(*dve_done.add("C1a", "x3", slots, s))

            pairs(dve, body_c1a)
            enter(dve, "C1b")
            nc.vector.memset(P8, -1.0).then_inc(degree_step, 1)
            dve.wait_ge(degree_step, 15)

            def body_c1b(i, slots):
                ph = "C1b"
                norm(ph, i, slots, lambda s: state(i, s))
                for s in slots:
                    if not first(i):
                        wait(dve, pe_done.done(ph, "zT", i - 1, s))
                    normed(s, ZT[s], state(i, s), 0)
                    normed(s, ZT[s], state(i, s), 1).then_inc(*dve_done.add(ph, "z", slots, s))

                def each(stage, needs, make, others=None):
                    for s in slots:
                        for x in needs:
                            self_wait(ph, x, i, s)
                        if others:
                            others(s)
                        make(s).then_inc(*dve_done.add(ph, stage, slots, s))

                def lg(s):
                    return LG[:, s, :, 0:NEXP1]

                def wide(x, s, n):
                    return x[:, s, :].rearrange("p (t u) -> p t u", u=1).to_broadcast([T, 2, n])

                def twice(f):
                    def make(s):
                        f(s, 0)
                        return f(s, 1)
                    return make

                each("logit", [], lambda s: nc.vector.tensor_tensor(
                    lg(s), PC[s][0:T, 0:16].rearrange("p (t e) -> p t e", t=2)[:, :, 0:NEXP1],
                    rowS[:].rearrange("p (u e) -> p u e", u=1).to_broadcast([T, 2, NEXP1]), ALU.add),
                    lambda s: wait(dve, pe_done.done(ph, "logit", i, s)))
                each("lmax", ["logit"], lambda s: nc.vector.tensor_reduce(LM[:, s, :], lg(s), AX.X, ALU.max))
                each("lsub", ["lmax"], lambda s: nc.vector.tensor_tensor(lg(s), lg(s), wide(LM, s, NEXP1), ALU.subtract))
                each("lsum", [], lambda s: nc.vector.tensor_reduce(LM[:, s, :], lg(s), AX.X, ALU.add),
                     lambda s: wait(dve, act_done.done(ph, "pexp", i, s)))
                each("lrec", ["lsum"], lambda s: nc.vector.reciprocal(LM[:, s, :], LM[:, s, :]))
                each("p", ["lrec"], lambda s: nc.vector.tensor_tensor(
                    P8[:, s, :, 0:NEXP1], lg(s), wide(LM, s, NEXP1), ALU.mult))
                each("max", ["p"], twice(lambda s, t: nc.vector.max(MX[:, s, t, :], P8[:, s, t, :])),
                     lambda s: hold(dve))
                each("arg", ["max"], twice(lambda s, t: nc.vector.max_index(
                    IX[:, s, t, :], MX[:, s, t, :], P8[:, s, t, :])), lambda s: hold(dve))
                each("argf", ["arg"], lambda s: nc.vector.tensor_copy(IXF[:, s, :, :], IX[:, s, :, :]))
                each("gdif", ["argf"], lambda s: nc.vector.tensor_tensor(
                    GD[:, s, :], MX[:, s, :, 1], MX[:, s, :, 0], ALU.subtract))
                each("gsum", [], lambda s: nc.vector.tensor_scalar(GA[:, s, :], GD[:, s, :], 1.0, None, ALU.add),
                     lambda s: wait(dve, act_done.done(ph, "gexp", i, s)))
                each("g1", ["gsum"], lambda s: nc.vector.reciprocal(GA[:, s, :], GA[:, s, :]))
                each("g2", ["g1"], lambda s: nc.vector.tensor_tensor(GB[:, s, :], GD[:, s, :], GA[:, s, :], ALU.mult))

                def choose(s, t):
                    nc.vector.tensor_scalar(G2[:, s, t, :], iota32[:, 0:8], IXF[:, s, t, 1:2], GB[:, s, t:t + 1],
                                            ALU.is_equal, ALU.mult)
                    return nc.vector.tensor_scalar(G1[:, s, t, :], iota32[:, 0:8], IXF[:, s, t, 0:1],
                                                   GA[:, s, t:t + 1], ALU.is_equal, ALU.mult)

                each("one", ["g2"], twice(choose))
                each("gate", ["one"], lambda s: nc.vector.tensor_tensor(
                    G1[:, s, :, :], G1[:, s, :, :], G2[:, s, :, :], ALU.add))
                each("yb", [], lambda s: nc.vector.tensor_tensor(KT[s], state(i, s), ptok(PA[s]), ALU.add),
                     lambda s: (wait(dve, pe_done.done(ph, "yb", i, s)),
                                None if first(i) else wait(dve, k_stored.done(ph, i - 1, s))))
                for e in range(NEXP1):
                    each(f"y{e}", [f"y{e - 1}" if e else "yb"], twice(
                        lambda s, t: nc.vector.scalar_tensor_tensor(
                            KT[s][:, t, :], ptok(PA[s])[:, t, :], G1[:, s, t, e:e + 1], KT[s][:, t, :],
                            ALU.mult, ALU.add)),
                         lambda s: wait(dve, pe_done.done(ph, f"o{e}" if e < NEXP1 - 1 else "out", i, s)))

            pairs(dve, body_c1b)

        @block.tensor
        def _(pe):
            def turn_tok(dst, source, n=2):
                for k in range(n):
                    for t in range(2):
                        ins = nc.tensor.transpose(dst[:, k, T * t:T * t + T], source[:, t, 128 * k:128 * k + 128],
                                                  ident[0:T, 0:T])
                return ins

            def tokens(dst, source, w, k0=0, k1=2, begin=True, end=True):
                for k in range(k0, k1):
                    for t in range(2):
                        ins = nc.tensor.matmul(dst[:, t, :], source[:, k, T * t:T * t + T], w[:, k, :],
                                               start=(begin and k == k0 and t == 0), stop=(end and k == k1 - 1),
                                               skip_group_check=True)
                return ins

            def hidden(dst, w, b0, sources):
                for b in range(2):
                    n = 0
                    for source, k0 in sources:
                        for k in range(2):
                            ins = nc.tensor.matmul(dst[:, b, :], w[:, k0 + k, 128 * (b0 + b):128 * (b0 + b) + 128],
                                                   source[:, k, :], start=(n == 0), stop=(n == 2 * len(sources) - 1))
                            n += 1
                return ins

            def sort_sums_of(e):
                pe.wait_ge(sort_step, e * SORT_STEPS + 9 + 4 * NT)
                nc.tensor.matmul(PA[1][0:T, 0:NT], ones[0:T, 0:T], tot, start=True, stop=True)
                nc.tensor.matmul(PB[1][0:T, 0:NT], lower[0:T, 0:T], tot, start=True, stop=True)
                nc.tensor.matmul(PC[1][0:NT, 0:1], tot, ones[0:T, 0:1], start=True, stop=True)\
                    .then_inc(sort_sums, 1)
                pe.wait_ge(sort_step, e * SORT_STEPS + 9 + 4 * NT + 7)
                nc.tensor.matmul(PA[1][0:NT, 0:1], lower[0:NT, 0:NT], grT[:], start=True, stop=True)\
                    .then_inc(sort_sums, 1)
                pe.wait_ge(sort_step, (e + 1) * SORT_STEPS - 1)
                nc.tensor.matmul(PB[1][0:1, 0:NG], ones[0:NT, 0:1], gcmp, start=True, stop=True)\
                    .then_inc(sort_sums, 1)

            def sum_groups(e, turn, g0, g1):
                for u in range(2 * g0, 2 * g1):
                    pe.wait_ge(gathered[u], turn * 16 + (16 * (e * NS // RING + 1)))
                    pe.wait_ge(onehot_made, turn * RING + (e * NS + u + 1))
                    if u % 2 == 0:
                        pe.wait_ge(group_added, turn * GROUPS + (e * NG + u // 2 + 1))
                    nc.tensor.matmul(PSUMS[u // 2 % 2][0:T, 0:D + 1], onehot[:, u, :], rows[:, u, :],
                                     start=(u % 2 == 0), stop=(u % 2 == 1)).then_inc(row_free, 1)

            def sum_groups_beside(phase, i, k, g0, g1):
                turn, n = turns(phase, i)
                if k < n:
                    sum_groups(1, turn + k, g0, g1)

            def sum_edges(e):
                with pe.Fori(0, NS // RING) as i:
                    sum_groups(e, i, 0, GROUPS)

            def begin(phase):
                if phase != "A0":
                    enter(pe, phase)
                if phase == "C0b":
                    pe.wait_ge(consts_made, 21)
                pe.wait_ge(weights_loaded[phase], weight_loads[phase])

            pe.wait_ge(consts_made, 18)
            pe.wait_ge(consts_loaded, 16 * (len(vectors) + 3))
            nc.tensor.transpose(PC[0][:, 0:n_cols], vector_rows, ident[0:n_cols, 0:n_cols])
            for k in range(2):
                ins = nc.tensor.transpose(PC[0][:, 128 + NEXP * k:128 + NEXP * k + NEXP], router_rows[:, k, :],
                                          ident[0:NEXP, 0:NEXP])
            ins.then_inc(consts_turned, 1)
            sort_sums_of(0)
            begin("A0")
            pe.wait_ge(consts_turned, 3)

            def body_a0(i, slots):
                for s in slots:
                    wait(pe, dve_done.done("A0", "z", i, s))
                    if not first(i):
                        wait(pe, dve_done.done("A0", "q", i - 1, s))
                    turn_tok(pfeat(PA[s]), ZT[s]).then_inc(*pe_done.add("A0", "zT", slots, s))
                for s in slots:
                    wait(pe, act_done.done("A0", "zT", i, s))
                    if not first(i):
                        wait(pe, dve_done.done("A0", "ctx", i - 1, s))
                    tokens(ptok(PB[s]), FT[s], wk).then_inc(*pe_done.add("A0", "k", slots, s))
                for s in slots:
                    if not first(i):
                        wait(pe, act_done.done("A0", "v", i - 1, s))
                    tokens(ptok(PC[s]), FT[s], wv).then_inc(*pe_done.add("A0", "v", slots, s))
                for s in slots:
                    tokens(ptok(PA[s]), FT[s], wq).then_inc(*pe_done.add("A0", "q", slots, s))
                for s in slots:
                    wait(pe, dve_done.done("A0", "k", i, s))
                    wait(pe, act_done.done("A0", "v", i, s))
                    add_context(PB[s], s).then_inc(*pe_done.add("A0", "ctx", slots, s))

            def add_context(dst, s):
                for k in range(2):
                    for t in range(2):
                        ins = nc.tensor.matmul(dst[:, 256 * k:256 * k + 129], KT[s][:, t, 128 * k:128 * k + 128],
                                               VT[:, s, t, k, :], start=(t == 0), stop=(t == 1))
                return ins

            pairs(pe, body_a0)

            def make_context(phase, w):
                wait(pe, context(phase, "masked"))
                wait(pe, act_done.done(phase, KINDS[kind(phase)]["act"][-1], NP - 1))
                if phase == "A0":
                    for k in range(2):
                        nc.tensor.matmul(PC[0][0:T, 128 * k:128 * k + 128], ones[:, 0:T], KD[:, k, :],
                                         start=True, stop=True)
                for k in range(2):
                    ins = nc.tensor.transpose(PA[0][:, 128 * k:128 * k + 128], CN[:, k, :], ident[:])
                ins.then_inc(context_step, 1)
                wait(pe, context(phase, "turned_out"))
                for k in range(2):
                    ins = nc.tensor.matmul(PB[0][:, D * k:D * k + D], CNT[:, k, :], w[:, k, :], start=True, stop=True)
                ins.then_inc(context_step, 1)

            pe.wait_ge(weights_loaded["B0"], weight_loads["B0"])
            make_context("A0", w0_m)
            begin("B0")
            wait(pe, context("A0", "cleared"))

            def body_b0(i, slots):
                for s in slots:
                    wait(pe, dve_done.done("B0", "q", i, s))
                    if not first(i):
                        wait(pe, dve_done.done("B0", "oz", i - 1, s))
                    turn_tok(pfeat(PA[s]), QT[s]).then_inc(*pe_done.add("B0", "qT", slots, s))
                for s in slots:
                    wait(pe, act_done.done("B0", "qT", i, s))
                    tokens(ptok(PB[s]), QF[s], MM).then_inc(*pe_done.add("B0", "msg", slots, s))
                for s in slots:
                    wait(pe, dve_done.done("B0", "m", i, s))
                    turn_tok(pfeat(PA[s]), TM[s]).then_inc(*pe_done.add("B0", "mT", slots, s))
                for h, P in enumerate((PB, PC)):
                    for s in slots:
                        if h == 0:
                            wait(pe, act_done.done("B0", "mT", i, s))
                            wait(pe, f_loaded.done("B0", i, s))
                        elif not first(i):
                            wait(pe, act_done.done("B0", "h1", i - 1, s))
                        hidden(pfeat(P[s]), w0_mix1, 2 * h, ((FT[s], 0), (QF[s], 2)))\
                            .then_inc(*pe_done.add("B0", f"h{h}", slots, s))
                for s in slots:
                    wait(pe, act_done.done("B0", "h1", i, s))
                    tokens(ptok(PA[s]), HT[:, s], w0_mix2, 0, 4).then_inc(*pe_done.add("B0", "out", slots, s))

            pairs(pe, body_b0)
            sort_sums_of(1)
            sum_edges(0)
            begin("C0a")

            def body_c0a(i, slots):
                for s in slots:
                    wait(pe, dve_done.done("C0a", "h", i, s))
                    if not first(i):
                        wait(pe, dve_done.done("C0a", "x1", i - 1, s))
                    turn_tok(pfeat(PA[s]), ZT[s]).then_inc(*pe_done.add("C0a", "hT", slots, s))
                for h, P in enumerate((PB, PC)):
                    for s in slots:
                        if h == 0:
                            wait(pe, act_done.done("C0a", "hT", i, s))
                        if not first(i):
                            wait(pe, act_done.done("C0a", f"h{h}", i - 1, s))
                        hidden(pfeat(P[s]), w0_gnn1, 2 * h, ((FT[s], 0),)).then_inc(*pe_done.add("C0a", f"h{h}", slots, s))
                for s in slots:
                    wait(pe, act_done.done("C0a", "h1", i, s))
                    tokens(ptok(PA[s]), HT[:, s], w0_gnn2, 0, 4).then_inc(*pe_done.add("C0a", "out", slots, s))

            pairs(pe, body_c0a)
            begin("C0b")

            def body_c0b(i, slots):
                for s in slots:
                    wait(pe, dve_done.done("C0b", "z", i, s))
                    if not first(i):
                        wait(pe, dve_done.done("C0b", "x2", i - 1, s))
                    turn_tok(pfeat(PA[s]), ZT[s]).then_inc(*pe_done.add("C0b", "zT", slots, s))
                for s in slots:
                    wait(pe, act_done.done("C0b", "zT", i, s))
                    if not first(i):
                        wait(pe, act_done.done("C0b", "h7", i - 1, s))
                    for k in range(2):
                        for t in range(2):
                            ins = nc.tensor.matmul(PC[s][0:T, NEXP * t:NEXP * t + NEXP], FT[s][:, k, T * t:T * t + T],
                                                   w0_router[:, k, :], start=(k == 0 and t == 0), stop=(k == 1),
                                                   skip_group_check=True)
                    ins.then_inc(*pe_done.add("C0b", "logit", slots, s))
                for s in slots:
                    wait(pe, dve_done.done("C0b", "one", i, s))
                    for t in range(2):
                        ins = nc.tensor.transpose(PB[s][0:NEXP, T * t:T * t + T], OH[:, s, t, :], ident[0:T, 0:T])
                    ins.then_inc(*pe_done.add("C0b", "oneT", slots, s))

                def up(p):
                    for s in slots:
                        if p == 0:
                            wait(pe, dve_done.done("C0b", "mask", i, s))
                        if p >= 2:
                            wait(pe, act_done.done("C0b", f"h{p - 2}", i, s))
                        P = pfeat((PB, PC)[p % 2][s])
                        for b in range(2):
                            j = 2 * p + b
                            for k in range(2):
                                nc.tensor.matmul(P[:, b, :], w0_up[:, k, 128 * j:128 * j + 128], FT[s][:, k, :],
                                                 start=(k == 0), stop=False)
                            ins = nc.tensor.matmul(P[:, b, :], select[:, 128 * j:128 * j + 128], OHM[:, s, :],
                                                   start=False, stop=True)
                        ins.then_inc(*pe_done.add("C0b", f"h{p}", slots, s))

                def down(p, stage):
                    for s in slots:
                        wait(pe, act_done.done("C0b", f"h{p}", i, s))
                        if p == 0:
                            for t in range(2):
                                nc.tensor.matmul(ptok(PA[s])[:, t, :], OHT[:, s, T * t:T * t + T], bexp0,
                                                 start=(t == 0), stop=False, skip_group_check=True)
                        for b in range(2):
                            j = 2 * p + b
                            for t in range(2):
                                ins = nc.tensor.matmul(ptok(PA[s])[:, t, :], HT[:, s, j % 8, T * t:T * t + T],
                                                       w0_down[:, j, :], start=False, stop=(j == 15),
                                                       skip_group_check=True)
                        ins.then_inc(*pe_done.add("C0b", stage, slots, s))

                up(0)
                for p in range(1, 8):
                    up(p)
                    down(p - 1, f"o{p - 1}")
                down(7, "out")

            pairs(pe, body_c0b)

            for n in range(LAYERS):
                def body_a1(i, slots, phase=f"A1.{n}"):
                    for s in slots:
                        wait(pe, dve_done.done(phase, "z", i, s))
                        if not first(i):
                            wait(pe, act_done.done(phase, "qT", i - 1, s))
                        turn_tok(pfeat(PA[s]), ZT[s]).then_inc(*pe_done.add(phase, "zT", slots, s))
                    for s in slots:
                        wait(pe, act_done.done(phase, "zT", i, s))
                        if not first(i):
                            wait(pe, dve_done.done(phase, "qsub", i - 1, s))
                        hidden(pfeat(PB[s]), wk, 0, ((FT[s], 0),)).then_inc(*pe_done.add(phase, "k", slots, s))
                    for s in slots:
                        if not first(i):
                            wait(pe, dve_done.done(phase, "ctx", i - 1, s))
                        tokens(ptok(PC[s]), FT[s], wv).then_inc(*pe_done.add(phase, "v", slots, s))
                    sum_groups_beside(phase, i, 0, 0, 2)
                    for s in slots:
                        wait(pe, act_done.done(phase, "kexp", i, s))
                        for t in range(2):
                            for k in range(2):
                                ins = nc.tensor.transpose(ptok(PA[s])[:, t, 128 * k:128 * k + 128],
                                                          PF[s][:, k, T * t:T * t + T], ident[:])
                        ins.then_inc(*pe_done.add(phase, "kT", slots, s))
                    for s in slots:
                        tokens(ptok(PB[s]), FT[s], wq).then_inc(*pe_done.add(phase, "q", slots, s))
                    for s in slots:
                        wait(pe, dve_done.done(phase, "kT", i, s))
                        wait(pe, act_done.done(phase, "v", i, s))
                        add_context(PC[s], s).then_inc(*pe_done.add(phase, "ctx", slots, s))
                    sum_groups_beside(phase, i, 0, 2, 4)
                    for s in slots:
                        wait(pe, dve_done.done(phase, "q", i, s))
                        turn_tok(pfeat(PA[s]), QT[s]).then_inc(*pe_done.add(phase, "qT", slots, s))

                begin(f"A1.{n}")
                pairs(pe, body_a1)
                make_context(f"A1.{n}", wo)
                begin(f"B1.{n}")
                wait(pe, context(f"A1.{n}", "cleared"))

                def body_b1(i, slots, phase=f"B1.{n}"):
                    for s in slots:
                        wait(pe, q_loaded.done(phase, i, s))
                        if not first(i):
                            wait(pe, dve_done.done(phase, "out", i - 1, s))
                        tokens(ptok(PA[s]), QF[s], MM).then_inc(*pe_done.add(phase, "att", slots, s))
                    sum_groups_beside(phase, i, 0, 0, 2)
                    for s in slots:
                        wait(pe, dve_done.done(phase, "z", i, s))
                        if not first(i):
                            wait(pe, act_done.done(phase, "h2", i - 1, s))
                        turn_tok(pfeat(PB[s]), ZT[s]).then_inc(*pe_done.add(phase, "zT", slots, s))

                    def up(p):
                        for s in slots:
                            if p == 0:
                                wait(pe, act_done.done(phase, "zT", i, s))
                            elif p == 1 and not first(i):
                                wait(pe, act_done.done(phase, "h3", i - 1, s))
                            elif p >= 2:
                                wait(pe, act_done.done(phase, f"h{p - 2}", i, s))
                            hidden(pfeat((PB, PC)[p % 2][s]), w1_up, 2 * p, ((FT[s], 0),))\
                                .then_inc(*pe_done.add(phase, f"h{p}", slots, s))

                    def down(p, stage):
                        for s in slots:
                            wait(pe, act_done.done(phase, f"h{p}", i, s))
                            tokens(ptok(PA[s]), HT[:, s], w1_down, 2 * p, 2 * p + 2, p == 0, p == 3)\
                                .then_inc(*pe_done.add(phase, stage, slots, s))

                    sum_groups_beside(phase, i, 0, 2, 4)
                    up(0)
                    up(1)
                    sum_groups_beside(phase, i, 1, 0, 2)
                    up(2)
                    down(0, "o0")
                    sum_groups_beside(phase, i, 1, 2, 4)
                    up(3)
                    down(1, "o1")
                    down(2, "o2")
                    down(3, "out")

                pairs(pe, body_b1)

            begin("C1a")

            def body_c1a(i, slots):
                for s in slots:
                    wait(pe, dve_done.done("C1a", "hs", i, s))
                    if not first(i):
                        wait(pe, dve_done.done("C1a", "x3", i - 1, s))
                    turn_tok(pfeat(PA[s]), ZT[s]).then_inc(*pe_done.add("C1a", "hT", slots, s))
                for s in slots:
                    wait(pe, act_done.done("C1a", "hT", i, s))
                    tokens(ptok(PA[s]), FT[s], w1_gnn).then_inc(*pe_done.add("C1a", "out", slots, s))

            pairs(pe, body_c1a)
            begin("C1b")

            def body_c1b(i, slots):
                ph = "C1b"
                for s in slots:
                    wait(pe, dve_done.done(ph, "z", i, s))
                    if not first(i):
                        wait(pe, dve_done.done(ph, f"y{NEXP1 - 1}", i - 1, s))
                    turn_tok(pfeat(PA[s]), ZT[s]).then_inc(*pe_done.add(ph, "zT", slots, s))
                for s in slots:
                    wait(pe, act_done.done(ph, "zT", i, s))
                    for k in range(2):
                        ins = nc.tensor.matmul(PB[s][:, 0:CH], w1_rh[:, k, :], FT[s][:, k, :], start=(k == 0), stop=(k == 1))
                    ins.then_inc(*pe_done.add(ph, "rh", slots, s))
                for s in slots:
                    wait(pe, act_done.done(ph, "rh", i, s))
                    for t in range(2):
                        ins = nc.tensor.matmul(PC[s][0:T, 8 * t:8 * t + NEXP1], QF[s][:, 0, T * t:T * t + T],
                                               w1_router[:, 0, :], start=True, stop=True)
                    ins.then_inc(*pe_done.add(ph, "logit", slots, s))
                for s in slots:
                    wait(pe, dve_done.done(ph, "gate", i, s))
                    for t in range(2):
                        ins = nc.tensor.transpose(PB[s][0:8, T * t:T * t + T], G1[:, s, t, :], ident[0:T, 0:T])
                    ins.then_inc(*pe_done.add(ph, "gT", slots, s))
                for s in slots:
                    wait(pe, act_done.done(ph, "gT", i, s))
                    for t in range(2):
                        ins = nc.tensor.matmul(ptok(PA[s])[:, t, :], GT[0:NEXP1, s, T * t:T * t + T], bexp1,
                                               start=(t == 0), stop=True, skip_group_check=True)
                    ins.then_inc(*pe_done.add(ph, "yb", slots, s))

                def first_layer(e):
                    for s in slots:
                        if e:
                            wait(pe, act_done.done(ph, f"a{e - 1}", i, s))
                        hidden(pfeat(PB[s]), w1_exp[0][e], 0, ((FT[s], 0),)).then_inc(*pe_done.add(ph, f"a{e}", slots, s))

                def second_layer(e):
                    for s in slots:
                        wait(pe, act_done.done(ph, f"a{e}", i, s))
                        if e:
                            wait(pe, act_done.done(ph, f"b{e - 1}", i, s))
                        hidden(pfeat(PC[s]), w1_exp[1][e], 0, ((HT[:, s, 4 * (e % 2):4 * (e % 2) + 2, :], 0),))\
                            .then_inc(*pe_done.add(ph, f"b{e}", slots, s))

                def third_layer(e, stage):
                    for s in slots:
                        wait(pe, act_done.done(ph, f"b{e}", i, s))
                        wait(pe, dve_done.done(ph, f"y{e - 1}" if e else "yb", i, s))
                        tokens(ptok(PA[s]), HT[:, s, 4 * (e % 2) + 2:4 * (e % 2) + 4, :], w1_exp[2][e])\
                            .then_inc(*pe_done.add(ph, stage, slots, s))

                first_layer(0)
                second_layer(0)
                for e in range(1, NEXP1):
                    first_layer(e)
                    third_layer(e - 1, f"o{e - 1}")
                    second_layer(e)
                third_layer(NEXP1 - 1, "out")

            pairs(pe, body_c1b)


def kernel(**inputs):
    import numpy as _np
    import concourse.bacc as _bacc
    from concourse import mybir as _mybir
    from concourse.bass_utils import run_bass_kernel_spmd as _run

    nc = _bacc.Bacc("TRN2", target_bir_lowering=False, num_devices=1)
    arrays, args = {}, {}
    for name, value in inputs.items():
        v = _np.ascontiguousarray(value)
        arrays[f"in_{name}"] = v
        args[name] = nc.dram_tensor(f"in_{name}", v.shape, _mybir.dt.from_np(v.dtype), kind="ExternalInput").ap()
    out = nc.dram_tensor("out_0", (N, D), F32, kind="ExternalOutput").ap()
    build(nc, args, out)
    r = _run(nc, [arrays], core_ids=[0])
    return r.results[0]["out_0"]
```
